# Optimizing a Trainium2 kernel written in Bass

```python
import numpy as np
import jax
import jax.numpy as jnp

def _softmax(x, axis=-1):
    return jax.nn.softmax(x, axis=axis)

def _gelu(x):
    return jax.nn.gelu(x, approximate=True)

def _silu(x):
    return jax.nn.silu(x)

def _sigmoid(x):
    return jax.nn.sigmoid(x)

def _layernorm(x, axis=-1, eps=1e-05):
    m = jnp.mean(x, axis=axis, keepdims=True)
    v = jnp.var(x, axis=axis, keepdims=True)
    return (x - m) / jnp.sqrt(v + eps)

def _scatter_add(tgt, idx, src, axis=0):
    return tgt.at[idx].add(src)

def _segment_sum(src, seg, n):
    return jax.ops.segment_sum(src, seg, n)
kernel_name = 'mk_decoder_postln_d1_seqx_r8_f940e2'

def setup_inputs(seed: int=0):
    np.random.seed(seed)
    _w = jnp.asarray

    def _rec_inputs():
        import jax
        import jax.numpy as jnp
        _rk = jax.random.key(seed)
        x = -0.0002928 + 1 * jax.random.normal(jax.random.fold_in(_rk, 1), (16, 128, 256), jnp.float32)
        _lenS = 128 - jax.random.randint(jax.random.fold_in(_rk, 7), (16,), 0, max(1, 128 // 4) + 1, jnp.int32)
        _lenS2 = 128 - jax.random.randint(jax.random.fold_in(_rk, 8), (16,), 0, max(1, 128 // 4) + 1, jnp.int32)
        fside_S2_0 = -0.00337071 + 1.01897 * jax.random.normal(jax.random.fold_in(_rk, 11), (128,), jnp.float32)
        _ctx_2048P = jax.random.normal(jax.random.fold_in(_rk, 12), (16, 16, 256), jnp.float32)
        _ctx_2048c = jax.random.dirichlet(jax.random.fold_in(_rk, 512), 0.3 * jnp.ones((16,), jnp.float32), (16, 128))
        _ctx_2048t = jnp.einsum('bsk,bkd->bsd', _ctx_2048c, _ctx_2048P)
        _ctx_2048t = _ctx_2048t * jax.lax.rsqrt(jnp.mean(jnp.square(_ctx_2048t)) + 1e-12) * 0.953939
        ctx_2048 = 0.000675642 + 1.00031 * (_ctx_2048t + 0.3 * jax.random.normal(jax.random.fold_in(_rk, 612), (16, 128, 256), jnp.float32))
        return (x, fside_S2_0, ctx_2048)
    x, fside_S2_0, ctx_2048 = _rec_inputs()

    def _L0_attn_setup():
        import jax, jax.numpy as jnp
        import numpy as np
        H = 16
        CHUNK = 64
        EPS = 1e-05

        def _forward(x, wq, wk, wv, wo, fq1_w, fq1_b, fq2_w, fq2_b, fk1_w, fk1_b, fk2_w, fk2_b, norm_w):
            B, L, D = x.shape
            dk = D // H

            def proj(w):
                return (x @ w.T).reshape(B, L, H, dk).transpose(0, 2, 1, 3)
            q, k, v = (proj(wq), proj(wk), proj(wv))
            q = (q @ fq1_w.T + fq1_b) * (q @ fq2_w.T + fq2_b)
            k = (k @ fk1_w.T + fk1_b) * (k @ fk2_w.T + fk2_b)
            scale = dk ** (-0.5)
            n = L // CHUNK
            qc = q.reshape(B, H, n, CHUNK, dk) * scale
            kc = k.reshape(B, H, n, CHUNK, dk)
            vc = v.reshape(B, H, n, CHUNK, dk)
            kv = jnp.einsum('bhncd,bhnce->bhnde', kc, vc)
            kv = jnp.cumsum(kv, axis=2)
            kv = jnp.concatenate([jnp.zeros_like(kv[:, :, :1]), kv[:, :, :-1]], axis=2)
            inter = jnp.einsum('bhncd,bhnde->bhnce', qc, kv)
            s = jnp.einsum('bhncd,bhnmd->bhncm', qc, kc)
            mask = jnp.tril(jnp.ones((CHUNK, CHUNK), bool))
            s = jnp.where(mask, s, 0.0)
            intra = jnp.einsum('bhncm,bhnmd->bhncd', s, vc)
            o = (inter + intra).reshape(B, H, L, dk)
            o = o * jax.lax.rsqrt(jnp.mean(o * o, axis=-1, keepdims=True) + EPS) * norm_w
            o = o.transpose(0, 2, 1, 3).reshape(B, L, D)
            return o @ wo.T
        key = jax.random.key(seed)
        ks = jax.random.split(key, 16)
        B, L, D = (2, 512, 256)
        dk = D // H
        g = 2 ** (-2.5)

        def xav(k, n):
            lim = g * np.sqrt(6.0 / (2 * n))
            return jax.random.uniform(k, (n, n), jnp.float32, -lim, lim)
        return {'x': jax.random.normal(ks[0], (B, L, D), jnp.float32), 'wq': xav(ks[1], D), 'wk': xav(ks[2], D), 'wv': xav(ks[3], D), 'wo': xav(ks[4], D), 'fq1_w': xav(ks[5], dk), 'fq1_b': jnp.zeros((dk,), jnp.float32), 'fq2_w': xav(ks[6], dk), 'fq2_b': jnp.zeros((dk,), jnp.float32), 'fk1_w': xav(ks[7], dk), 'fk1_b': jnp.zeros((dk,), jnp.float32), 'fk2_w': xav(ks[8], dk), 'fk2_b': jnp.zeros((dk,), jnp.float32), 'norm_w': jnp.ones((dk,), jnp.float32)}
    _L0_attn_all = _L0_attn_setup()
    _L0_attn_in = {k: v for k, v in _L0_attn_all.items() if k in ('wq', 'wk', 'wv', 'wo', 'fq1_w', 'fq1_b', 'fq2_w', 'fq2_b', 'fk1_w', 'fk1_b', 'fk2_w', 'fk2_b', 'norm_w')}
    del _L0_attn_all

    def _L0_xattn_setup():
        import jax, jax.numpy as jnp
        import numpy as np
        key = jax.random.key(seed)
        ks = jax.random.split(key, 5)
        B, D, L, NH = (2, 128, 256, 8)
        H = D // NH
        return {'v': jax.random.normal(ks[0], (B, D, L), jnp.float32), 'k': jax.random.normal(ks[1], (H, L), jnp.float32) * 0.1, 'bias': jax.random.normal(ks[2], (D,), jnp.float32), 'x1': jax.random.normal(ks[3], (B, D, L), jnp.float32), 'x2': jax.random.normal(ks[4], (B, D, L), jnp.float32), 'num_heads': NH}
    _L0_xattn_all = _L0_xattn_setup()
    _L0_xattn_in = {k: v for k, v in _L0_xattn_all.items() if k in ('k',)}
    del _L0_xattn_all

    def _L0_ffn_setup():
        import jax, jax.numpy as jnp
        import numpy as np
        BLOCK_SIZE = 32
        HIDDEN_SIZE = 256
        MLP_DIM = 2048
        NVFP4_LUT = jnp.array([0.0, 0.5, 1.0, 1.5, 2.0, 3.0, 4.0, 6.0, 0.0, -0.5, -1.0, -1.5, -2.0, -3.0, -4.0, -6.0], dtype=jnp.float32)

        def dequant_nvfp4(W_packed, scales, block=BLOCK_SIZE):
            N = W_packed.shape[0]
            low = W_packed & 15
            high = W_packed >> 4 & 15
            idx = jnp.stack([low, high], axis=-1).reshape(N, -1)
            vals = NVFP4_LUT[idx]
            K = vals.shape[1]
            vals = vals.reshape(N, K // block, block) * scales[:, :, None]
            return vals.reshape(N, K)
        key = jax.random.key(seed)
        ks = jax.random.split(key, 7)
        x = jax.random.normal(ks[0], (4, 32, HIDDEN_SIZE), dtype=jnp.float32)
        gate_W_packed = jax.random.randint(ks[1], (MLP_DIM, HIDDEN_SIZE // 2), 0, 32, dtype=jnp.int32)
        gate_scales = jax.random.uniform(ks[2], (MLP_DIM, HIDDEN_SIZE // BLOCK_SIZE), dtype=jnp.float32) * 0.1 + 0.001
        up_W_packed = jax.random.randint(ks[3], (MLP_DIM, HIDDEN_SIZE // 2), 0, 32, dtype=jnp.int32)
        up_scales = jax.random.uniform(ks[4], (MLP_DIM, HIDDEN_SIZE // BLOCK_SIZE), dtype=jnp.float32) * 0.1 + 0.001
        down_W_packed = jax.random.randint(ks[5], (HIDDEN_SIZE, MLP_DIM // 2), 0, 32, dtype=jnp.int32)
        down_scales = jax.random.uniform(ks[6], (HIDDEN_SIZE, MLP_DIM // BLOCK_SIZE), dtype=jnp.float32) * 0.1 + 0.001
        return {'x': x, 'gate_W_packed': gate_W_packed, 'gate_scales': gate_scales, 'up_W_packed': up_W_packed, 'up_scales': up_scales, 'down_W_packed': down_W_packed, 'down_scales': down_scales}
    _L0_ffn_all = _L0_ffn_setup()
    _L0_ffn_in = {k: v for k, v in _L0_ffn_all.items() if k in ('gate_W_packed', 'gate_scales', 'up_W_packed', 'up_scales', 'down_W_packed', 'down_scales')}
    del _L0_ffn_all
    return {'x': x, 'fside_S2_0': fside_S2_0, 'ctx_2048': ctx_2048, 'L0_attn_wq': _L0_attn_in['wq'], 'L0_attn_wk': _L0_attn_in['wk'], 'L0_attn_wv': _L0_attn_in['wv'], 'L0_attn_wo': _L0_attn_in['wo'], 'L0_attn_fq1_w': _L0_attn_in['fq1_w'], 'L0_attn_fq1_b': _L0_attn_in['fq1_b'], 'L0_attn_fq2_w': _L0_attn_in['fq2_w'], 'L0_attn_fq2_b': _L0_attn_in['fq2_b'], 'L0_attn_fk1_w': _L0_attn_in['fk1_w'], 'L0_attn_fk1_b': _L0_attn_in['fk1_b'], 'L0_attn_fk2_w': _L0_attn_in['fk2_w'], 'L0_attn_fk2_b': _L0_attn_in['fk2_b'], 'L0_attn_norm_w': _L0_attn_in['norm_w'], 'L0_xattn_k': _L0_xattn_in['k'], 'L0_ffn_gate_W_packed': _L0_ffn_in['gate_W_packed'], 'L0_ffn_gate_scales': _L0_ffn_in['gate_scales'], 'L0_ffn_up_W_packed': _L0_ffn_in['up_W_packed'], 'L0_ffn_up_scales': _L0_ffn_in['up_scales'], 'L0_ffn_down_W_packed': _L0_ffn_in['down_W_packed'], 'L0_ffn_down_scales': _L0_ffn_in['down_scales']}

def reference(x, fside_S2_0, ctx_2048, L0_attn_wq, L0_attn_wk, L0_attn_wv, L0_attn_wo, L0_attn_fq1_w, L0_attn_fq1_b, L0_attn_fq2_w, L0_attn_fq2_b, L0_attn_fk1_w, L0_attn_fk1_b, L0_attn_fk2_w, L0_attn_fk2_b, L0_attn_norm_w, L0_xattn_k, L0_ffn_gate_W_packed, L0_ffn_gate_scales, L0_ffn_up_W_packed, L0_ffn_up_scales, L0_ffn_down_W_packed, L0_ffn_down_scales):
    import jax
    import jax.numpy as jnp

    def _L0_attn_ref(x, wq, wk, wv, wo, fq1_w, fq1_b, fq2_w, fq2_b, fk1_w, fk1_b, fk2_w, fk2_b, norm_w):
        import jax, jax.numpy as jnp
        import numpy as np
        H = 16
        CHUNK = 64
        EPS = 1e-05

        def _forward(x, wq, wk, wv, wo, fq1_w, fq1_b, fq2_w, fq2_b, fk1_w, fk1_b, fk2_w, fk2_b, norm_w):
            B, L, D = x.shape
            dk = D // H

            def proj(w):
                return (x @ w.T).reshape(B, L, H, dk).transpose(0, 2, 1, 3)
            q, k, v = (proj(wq), proj(wk), proj(wv))
            q = (q @ fq1_w.T + fq1_b) * (q @ fq2_w.T + fq2_b)
            k = (k @ fk1_w.T + fk1_b) * (k @ fk2_w.T + fk2_b)
            scale = dk ** (-0.5)
            n = L // CHUNK
            qc = q.reshape(B, H, n, CHUNK, dk) * scale
            kc = k.reshape(B, H, n, CHUNK, dk)
            vc = v.reshape(B, H, n, CHUNK, dk)
            kv = jnp.einsum('bhncd,bhnce->bhnde', kc, vc)
            kv = jnp.cumsum(kv, axis=2)
            kv = jnp.concatenate([jnp.zeros_like(kv[:, :, :1]), kv[:, :, :-1]], axis=2)
            inter = jnp.einsum('bhncd,bhnde->bhnce', qc, kv)
            s = jnp.einsum('bhncd,bhnmd->bhncm', qc, kc)
            mask = jnp.tril(jnp.ones((CHUNK, CHUNK), bool))
            s = jnp.where(mask, s, 0.0)
            intra = jnp.einsum('bhncm,bhnmd->bhncd', s, vc)
            o = (inter + intra).reshape(B, H, L, dk)
            o = o * jax.lax.rsqrt(jnp.mean(o * o, axis=-1, keepdims=True) + EPS) * norm_w
            o = o.transpose(0, 2, 1, 3).reshape(B, L, D)
            return o @ wo.T
        return _forward(x, wq, wk, wv, wo, fq1_w, fq1_b, fq2_w, fq2_b, fk1_w, fk1_b, fk2_w, fk2_b, norm_w)

    def _L0_xattn_ref(v, k, bias, x1, x2, num_heads):
        import jax, jax.numpy as jnp
        import numpy as np
        B, D, L = v.shape
        H = D // num_heads
        fft_size = 2 * L
        vr = v.reshape(B, H, num_heads, L)
        x1r = x1.reshape(B, H, num_heads, L)
        x2r = x2.reshape(B, H, num_heads, L)
        kv = vr[:, :, :, None, :] * x2r[:, :, None, :, :]
        k_f = jnp.fft.rfft(k.astype(jnp.float32), n=fft_size)
        y = jnp.fft.irfft(jnp.fft.rfft(kv, n=fft_size) * k_f[None, :, None, None, :], n=fft_size)[..., :L]
        skip = bias.astype(jnp.float32).reshape(H, num_heads)[None, :, :, None, None]
        y = y + kv * skip
        out = jnp.einsum('bhijl,bhil->bhjl', y, x1r)
        return out.reshape(B, D, L)

    def _L0_ffn_ref(x, gate_W_packed, gate_scales, up_W_packed, up_scales, down_W_packed, down_scales):
        import jax, jax.numpy as jnp
        import numpy as np
        BLOCK_SIZE = 32
        HIDDEN_SIZE = 256
        MLP_DIM = 2048
        NVFP4_LUT = jnp.array([0.0, 0.5, 1.0, 1.5, 2.0, 3.0, 4.0, 6.0, 0.0, -0.5, -1.0, -1.5, -2.0, -3.0, -4.0, -6.0], dtype=jnp.float32)

        def dequant_nvfp4(W_packed, scales, block=BLOCK_SIZE):
            N = W_packed.shape[0]
            low = W_packed & 15
            high = W_packed >> 4 & 15
            idx = jnp.stack([low, high], axis=-1).reshape(N, -1)
            vals = NVFP4_LUT[idx]
            K = vals.shape[1]
            vals = vals.reshape(N, K // block, block) * scales[:, :, None]
            return vals.reshape(N, K)
        B, S, H = x.shape
        xt = x.reshape(B * S, H)
        Wg = dequant_nvfp4(gate_W_packed, gate_scales)
        Wu = dequant_nvfp4(up_W_packed, up_scales)
        Wd = dequant_nvfp4(down_W_packed, down_scales)
        gate = jnp.einsum('th,nh->tn', xt, Wg)
        up = jnp.einsum('th,nh->tn', xt, Wu)
        gelu = jnp.tanh(0.7978845608028654 * (gate + 0.044715 * gate ** 3)) * gate * 0.5 + gate * 0.5
        inter = gelu * up
        out = jnp.einsum('tn,hn->th', inter, Wd)
        return out.reshape(B, S, H)
    x = _layernorm(x + _L0_attn_ref(x, L0_attn_wq, L0_attn_wk, L0_attn_wv, L0_attn_wo, L0_attn_fq1_w, L0_attn_fq1_b, L0_attn_fq2_w, L0_attn_fq2_b, L0_attn_fk1_w, L0_attn_fk1_b, L0_attn_fk2_w, L0_attn_fk2_b, L0_attn_norm_w), axis=-1)
    x = _layernorm(x + _L0_xattn_ref(x, L0_xattn_k, fside_S2_0, ctx_2048, ctx_2048, 8), axis=-1)
    x = _layernorm(x + _L0_ffn_ref(x, L0_ffn_gate_W_packed, L0_ffn_gate_scales, L0_ffn_up_W_packed, L0_ffn_up_scales, L0_ffn_down_W_packed, L0_ffn_down_scales), axis=-1)
    return x

_drawn_inputs = setup_inputs


def setup_inputs(seed=0):
    import zlib

    import numpy as np

    out = dict(_drawn_inputs(seed))
    spreads = {'L0_attn_fq1_b': (0.0, 0.646),
     'L0_attn_fq2_b': (0.0, 0.615),
     'L0_attn_fk1_b': (0.0, 0.565),
     'L0_attn_fk2_b': (0.0, 0.736),
     'L0_attn_norm_w': (1.0, 0.6)}
    factors = {'L0_attn_wq': 8.0,
     'L0_attn_wk': 6.078,
     'L0_attn_wv': 4.17,
     'L0_attn_wo': 4.151,
     'L0_attn_fq1_w': 7.123,
     'L0_attn_fq2_w': 8.0,
     'L0_attn_fk1_w': 8.0,
     'L0_attn_fk2_w': 5.656}
    for name, (base, spread) in spreads.items():
        noise = np.random.default_rng([zlib.crc32(name.encode()), seed]).standard_normal(out[name].shape)
        drawn = base * np.exp(spread * noise) if base else spread * noise
        out[name] = jnp.asarray(drawn.astype(out[name].dtype))
    for name, factor in factors.items():
        out[name] = (out[name] * factor).astype(out[name].dtype)
    return out
```

```python
import concourse.bass as bass
from concourse import mybir
from contextlib import ExitStack

F32 = mybir.dt.float32
F32R = mybir.dt.float32r
I32 = mybir.dt.int32
ALU = mybir.AluOpType
ACT = mybir.ActivationFunctionType
AX = mybir.AxisListType

P = 128
B, S, D = 16, 128, 256
H, DK = 16, 16
NB = 4
G = B // NB
T = NB * S
KT = D // P
HT = 8
CH, CI = 16, 8
F = 2048
NT = F // P
QC = 256
NQ = F // QC
LN_EPS = 1e-5
RMS_EPS = 1e-5


def count(eng, sem, per_group, g, k):
    value = per_group * g + k
    if isinstance(value, int) and value <= 0:
        return
    eng.wait_ge(sem, value)


def decoder_layer(nc, x, xT, ctx, ctxT, wq, wk, wvT, woT, fT, bias, skip, toep,
                  gate_p, gate_s, up_p, up_s, down_p, down_s, out):
    x_v = x.rearrange("b t f -> t b f")
    out_v = out.rearrange("b t f -> t b f")
    ctx_v = ctx.rearrange("b t f -> t b f")
    xT_v = xT.rearrange("(k p) t -> p k t", p=P)
    ctxT_v = ctxT.rearrange("(k p) t -> p k t", p=P)

    with ExitStack() as stack:
        def sb(name, shape, dt=F32):
            return stack.enter_context(nc.sbuf_tensor(name, shape, dt))

        def sem(name):
            return stack.enter_context(nc.semaphore(name))

        fold_w = sb("fold_w", [P, 4, KT, D])
        wv_sb = sb("wv_sb", [P, KT, D])
        wo_sb = sb("wo_sb", [P, KT, D])
        ffn_hi = sb("ffn_hi", [P, 3, 2, F], F32R)
        ffn_lo = sb("ffn_lo", [P, 3, 2, F], F32R)
        toep_sb = sb("toep_sb", [P, CH, 2 * P])
        ident = sb("ident", [P, P])
        causal = sb("causal", [P, P])
        head_one = sb("head_one", [P, HT, DK])
        skip_mat = sb("skip_mat", [P, CH, CI])
        head_sel = sb("head_sel", [P, HT])
        f_small = sb("f_small", [P, 4, DK])
        b_small = sb("b_small", [P, 6])
        skip_sb = sb("skip_sb", [P, 1])
        minus_half = sb("minus_half", [P, 1])
        act_bias = sb("act_bias", [P, 2])
        xT_sb = sb("xT_sb", [P, KT, T])
        x1T_sb = sb("x1T_sb", [P, KT, T])
        conv_sb = sb("conv_sb", [P, KT, NB, S])
        x_sb = sb("x_sb", [P, NB, D])
        ctxT_sb = sb("ctxT_sb", [P, KT, T])
        gate_q = sb("gate_q", [P, 2, T])
        o_sb = gate_q
        qT_sb = sb("qT_sb", [P, KT, T])
        rms_sb = qT_sb
        kT_sb = sb("kT_sb", [P, KT, T])
        fac_sb = prod_sb = kT_sb
        sc_sb = sb("sc_sb", [P, 2, 4, P])
        v_sb = sb("v_sb", [P, NB, HT, 3 * DK])
        ctx_sb = sb("ctx_sb", [P, NB, D])
        inv_rms = sb("inv_rms", [P, NB * H])
        ve = sb("ve", [P, 3, NB])
        st = sb("st", [P, 3, NB, 6])
        mv = sb("mv", [P, 3, NB, 2])
        x2_sb = sb("x2_sb", [P, NB, D])
        qbd = sb("qbd", [P, 4, T])
        kv_sb = qbd[:, 0:2, :]
        z_sb = qbd[:, 2:4, :]

        psum = [stack.enter_context(nc.psum_tensor(f"bank{i}", [P, T], F32)) for i in range(8)]
        fb = psum[0:4]
        gate_ps, up_ps = psum[4], psum[5]
        down_ps = psum[6:8]

        def sems(*names):
            return [sem(n) for n in names]

        ld_fold, ld_wo, ld_toep, ld_small, ld_xT, ld_x, ld_ctxT, ld_ctx, stored = sems(
            "ld_fold", "ld_wo", "ld_toep", "ld_small", "ld_xT", "ld_x", "ld_ctxT", "ld_ctx", "stored")
        ld_w = sems("ld_w_even", "ld_w_odd")
        fold_mm, proj_mm, v_mm, s_mm, o_mm, ms_mm, rT_mm, wo_mm, x1T_mm = sems(
            "fold_mm", "proj_mm", "v_mm", "s_mm", "o_mm", "ms_mm", "rT_mm", "wo_mm", "x1T_mm")
        y_mm, cT_mm, skip_mm, x2T_mm, gate_mm, up_mm, down_mm = sems(
            "y_mm", "cT_mm", "skip_mm", "x2T_mm", "gate_mm", "up_mm", "down_mm")
        fold_ready, q2_ready, v_ready, sq_ready, wide_ready, rT_ready, x1T_ready = sems(
            "fold_ready", "q2_ready", "v_ready", "sq_ready", "wide_ready", "rT_ready", "x1T_ready")
        x2hi_ready, gelu_ready, ihi_ready, relu_ready, whi_ready = sems(
            "x2hi_ready", "gelu_ready", "ihi_ready", "relu_ready", "whi_ready")
        dve_const, bd_ready, qk_ready, qbd_ready, sm_ready, on_ready, z_ready, conv_ready = sems(
            "dve_const", "bd_ready", "qk_ready", "qbd_ready", "sm_ready", "on_ready", "z_ready", "conv_ready")
        ms_ready, half_ready, sk_ready, x2lo_ready, inter_ready = sems(
            "ms_ready", "half_ready", "sk_ready", "x2lo_ready", "inter_ready")
        code_ready, sign_ready, scale_ready, sum4_ready, wlo_ready = sems(
            "code_ready", "sign_ready", "scale_ready", "sum4_ready", "wlo_ready")
        y_ready, st_ready, mv_ready, ve_ready, ln_ready = (
            sems(*[f"{n}{i}" for i in (1, 2, 3)]) for n in ("y_ready", "st_ready", "mv_ready", "ve_ready", "ln_ready"))
        x1_ready, x2_ready, res_ready = ln_ready
        filled, const_ready, pool_mask, rms_ready, kv_ready, prod_ready, ilo_ready, sum6_ready, deq_ready = sems(
            "filled", "const_ready", "pool_mask", "rms_ready", "kv_ready", "prod_ready", "ilo_ready",
            "sum6_ready", "deq_ready")
        rstd_ready = sems("rstd_ready1", "rstd_ready2", "rstd_ready3")

        with ExitStack() as early:
            def sbe(name, shape, dt=F32):
                return early.enter_context(nc.sbuf_tensor(name, shape, dt))
            raw_w = sbe("raw_w", [P, 2, QC], I32)
            raw_s = sbe("raw_s", [P, 2, QC])
            code = sbe("code", [P, 2, QC], I32)
            sign = sbe("sign", [P, QC], I32)
            sgn_scale = sbe("sgn_scale", [P, 2, QC])
            relu4 = sbe("relu4", [P, 2, QC])
            relu6 = sbe("relu6", [P, 2, QC])
            weight = sbe("weight", [P, 2, QC])
        x2T_hi = sb("x2T_hi", [P, 2, T], F32R)
        x2T_lo = sb("x2T_lo", [P, 2, T], F32R)
        inter = sb("inter", [P, T])
        inter_hi = sb("inter_hi", [P, 2, T], F32R)
        inter_lo = sb("inter_lo", [P, 2, T], F32R)
        raw_q = ctxT_sb
        raw_k = x1T_sb
        f_bd = conv_sb[:].rearrange("p k b s -> p (k b) s")[:, 0:4, :]
        raw_wq = raw_q[:].rearrange("p k (a n) -> p (k a) n", n=D)[:, 0:KT, :]
        raw_wk = raw_k[:].rearrange("p k (a n) -> p (k a) n", n=D)[:, 0:KT, :]

        def channels(tile, kt, h):
            return tile[:, kt, :].rearrange("p (b c) -> p b c", c=S)[:, :, h * CI:(h + 1) * CI]

        def pairs(tile, i):
            return tile[:, i, :].rearrange("p (k b j i) -> p k b j i", k=KT, b=NB, i=CI)

        units = [(m, c) for m in range(3) for c in range(NQ)]
        NU = 2 * len(units)
        UPS = -(-NU // NT)

        packed = [(gate_p, gate_s), (up_p, up_s), (down_p, down_s)]
        slots = [[] for _ in range(NT)]
        slots[0] = [("proj", 0), ("proj", 1)]
        slots[1] = [("proj", 2), ("proj", 3), ("qbd", 0)]
        slots[2] = [("vproj", 0), ("proj", 4), ("proj", 5)]
        slots[3] = [("vproj", 1), ("proj", 6), ("proj", 7)]
        scores = [("score", u) for u in range(16)]
        slots[4] = scores[0:4] + [("qbd", 1)]
        slots[5] = scores[4:8] + [("qbd", 2)]
        slots[6] = scores[8:12] + [("qbd", 3)]
        slots[7] = scores[12:16] + [("score", 16), ("square", 0), ("square", 1)]
        slots[8] = [("rms", 0)]
        slots[9] = [("outproj", 0), ("outproj", 1)]
        slots[10] = [("x1T", 0)]
        slots[11] = [("conv", h) for h in range(0, 4)]
        slots[12] = [("conv", h) for h in range(4, 7)]
        slots[13] = [("conv", h) for h in range(7, 10)]
        slots[14] = [("conv", h) for h in range(10, 13)]
        slots[15] = [("conv", h) for h in range(13, 16)]

        def run(stages, g, slot):
            for name, k in slots[slot]:
                if name in stages:
                    stages[name](g, k)

        def schedule(eng, front, finish, ffn, tail, unpack):
            for s in range(NT):
                for n in range(UPS * s, UPS * (s + 1)):
                    unpack(n)
                run(front, 0, s)
            for n in range(UPS * NT, NU + 2):
                unpack(n)
            finish(0)
            with eng.Fori(1, G) as g:
                for s in range(NT):
                    ffn(g - 1, s)
                    run(front, g, s)
                tail(g - 1)
                finish(g)
            for s in range(NT):
                ffn(G - 1, s)
            tail(G - 1)

        block = stack.enter_context(nc.Block())

        @block.sync
        def _(sp):
            def load(g):
                tok, seq = (g * T, g * NB) if isinstance(g, int) else (sp.snap(g * T), sp.snap(g * NB))
                count(sp, proj_mm, 8, g, 0)
                sp.dma_start(xT_sb[:], xT_v[:, :, bass.ds(tok, T)]).then_inc(ld_xT, 16)
                if isinstance(g, int):
                    sp.wait_ge(fold_mm, 4)
                count(sp, z_ready, 16, g, 0)
                sp.dma_start(ctxT_sb[:], ctxT_v[:, :, bass.ds(tok, T)]).then_inc(ld_ctxT, 16)
                count(sp, x2_ready, NB, g, 0)
                sp.dma_start(x_sb[:], x_v[:, bass.ds(seq, NB), :]).then_inc(ld_x, 16)
                sp.dma_start(ctx_sb[:], ctx_v[:, bass.ds(seq, NB), :]).then_inc(ld_ctx, 16)

            def store(g):
                at = sp.snap(g * NB) if not isinstance(g, int) else g * NB
                count(sp, res_ready, NB, g, NB)
                sp.dma_start(out_v[:, bass.ds(at, NB), :], x2_sb[:]).then_inc(stored, 16)

            sp.dma_start(f_small[:], fT.rearrange("n p e -> p n e")).then_inc(ld_small, 16)
            sp.dma_start(b_small[:, 0:5], bias).then_inc(ld_small, 16)
            sp.dma_start(skip_sb[:], skip).then_inc(ld_small, 16)
            sp.dma_start(raw_wq, wq.rearrange("(k p) n -> p k n", p=P)).then_inc(ld_fold, 16)
            sp.dma_start(raw_wk, wk.rearrange("(k p) n -> p k n", p=P)).then_inc(ld_fold, 16)
            sp.dma_start(wv_sb[:], wvT.rearrange("(k p) n -> p k n", p=P)).then_inc(ld_wo, 16)
            sp.dma_start(wo_sb[:], woT.rearrange("(k p) n -> p k n", p=P)).then_inc(ld_wo, 16)
            load(0)
            sp.dma_start(toep_sb[:], toep.rearrange("h p n -> p h n")).then_inc(ld_toep, 16)
            with sp.Fori(1, G) as g:
                load(g)
                store(g - 1)
            store(G - 1)
            sp.wait_ge(stored, 16 * G)

        @block.gpsimd
        def _(pool):
            def fetch(u):
                m, c = units[u]
                codes, scales = packed[m]
                pool.dma_start(raw_w[:, u % 2, :], codes[:, c * QC:(c + 1) * QC]).then_inc(ld_w[u % 2], 16)
                src = scales[:, c * QC:(c + 1) * QC].unsqueeze(1).broadcast_to([HT, P // HT, QC])
                pool.dma_start(raw_s[:, u % 2, :], src).then_inc(ld_w[u % 2], 16)

            fetch(0)
            fetch(1)
            nc.gpsimd.memset(ident[:], 0.0).then_inc(filled, 1)
            nc.gpsimd.memset(causal[:], 1.0).then_inc(filled, 1)
            nc.gpsimd.memset(head_one[:], 1.0).then_inc(filled, 1)
            nc.gpsimd.memset(skip_mat[:], 1.0).then_inc(filled, 1)
            nc.gpsimd.memset(minus_half[:], -0.5).then_inc(filled, 1)
            nc.gpsimd.memset(v_sb[:], 0.0).then_inc(filled, 1)
            nc.gpsimd.memset(act_bias[:, 0:1], -0.5).then_inc(filled, 1)
            nc.gpsimd.memset(act_bias[:, 1:2], -1.5).then_inc(filled, 1)
            pool.wait_ge(filled, 8)
            masks = ((head_one, HT, DK), (skip_mat, CH, CI))
            for tile, n, w in masks:
                nc.gpsimd.affine_select(out=tile[:], in_=tile[:], compare_op=ALU.is_ge, fill=0.0, base=0,
                                        pattern=[[-w, n], [0, w]], channel_multiplier=1).then_inc(pool_mask, 1)
            pool.wait_ge(pool_mask, 2)
            for tile, n, w in masks:
                nc.gpsimd.affine_select(out=tile[:], in_=tile[:], compare_op=ALU.is_ge, fill=0.0, base=w - 1,
                                        pattern=[[w, n], [0, w]], channel_multiplier=-1).then_inc(const_ready, 1)
            nc.gpsimd.affine_select(out=ident[:], in_=ident[:], compare_op=ALU.not_equal, fill=1.0,
                                    base=0, pattern=[[-1, P]], channel_multiplier=1).then_inc(const_ready, 1)
            nc.gpsimd.affine_select(out=causal[:], in_=causal[:], compare_op=ALU.is_ge, fill=0.0,
                                    base=0, pattern=[[1, P]], channel_multiplier=-1).then_inc(const_ready, 1)

            def unpack(step):
                n = step - 1
                if n < 0 or n >= NU:
                    return
                pool.wait_ge(relu_ready, 2 * n + 2)
                pool.wait_ge(sum4_ready, n + 1)
                nc.gpsimd.tensor_tensor(relu6[:, n % 2], relu4[:, n % 2], relu6[:, n % 2], ALU.subtract)\
                    .then_inc(sum6_ready, 1)
                pool.wait_ge(sum6_ready, n + 1)
                pool.wait_ge(scale_ready, n + 1)
                if n >= 2:
                    pool.wait_ge(whi_ready, n - 1)
                    pool.wait_ge(wlo_ready, n - 1)
                nc.gpsimd.tensor_tensor(weight[:, n % 2], relu6[:, n % 2], sgn_scale[:, n % 2], ALU.mult)\
                    .then_inc(deq_ready, 1)
                if n % 2 and n // 2 + 2 < len(units):
                    fetch(n // 2 + 2)

            def rms(g, _):
                count(pool, ms_ready, 1, g, 1)
                nc.gpsimd.tensor_tensor(inv_rms[:], inv_rms[:], minus_half[:].broadcast_to([P, NB * H]),
                                        ALU.pow).then_inc(rms_ready, 1)

            def rstd(g, ln):
                count(pool, ve_ready[ln], 2, g, 2)
                nc.gpsimd.tensor_tensor(ve[:, ln, :], ve[:, ln, :], minus_half[:].broadcast_to([P, NB]),
                                        ALU.pow).then_inc(rstd_ready[ln], 1)

            def outproj(g, j):
                if j == 1:
                    rstd(g, 0)

            def x1T(g, _):
                count(pool, x1_ready, NB, g, NB)
                count(pool, ld_ctx, 16, g, 16)
                count(pool, s_mm, 16, g, 16)
                nc.gpsimd.tensor_tensor(prod_sb[:].rearrange("p k t -> p (k t)"),
                                        x_sb[:].rearrange("p b f -> p (b f)"),
                                        ctx_sb[:].rearrange("p b f -> p (b f)"), ALU.mult).then_inc(prod_ready, 1)

            def conv(g, h):
                if h == 0:
                    count(pool, ld_ctxT, 16, g, 16)
                    count(pool, x1T_ready, 2, g, 2)
                    count(pool, s_mm, 16, g, 16)
                if h >= 2:
                    count(pool, y_mm, 16, g, h - 1)
                for kt in range(KT):
                    v_i = channels(x1T_sb, kt, h).unsqueeze(2).broadcast_to([P, NB, CI, CI])
                    c_j = channels(ctxT_sb, kt, h).unsqueeze(3).broadcast_to([P, NB, CI, CI])
                    nc.gpsimd.tensor_tensor(pairs(kv_sb, h % 2)[:, kt], v_i, c_j, ALU.mult).then_inc(kv_ready, 1)

            def finish(g):
                rstd(g, 1)

            def ffn(g, n):
                count(pool, ihi_ready, NT, g, n + 1)
                if n >= 2:
                    count(pool, down_mm, NT, g, n - 1)
                nc.gpsimd.tensor_tensor(inter_lo[:, n % 2, :], inter[:], inter_hi[:, n % 2, :].bitcast(F32),
                                        ALU.subtract).then_inc(ilo_ready, 1)

            def tail(g):
                rstd(g, 2)

            schedule(pool, {"rms": rms, "outproj": outproj, "x1T": x1T, "conv": conv}, finish, ffn, tail, unpack)

        @block.scalar
        def _(act):
            for i in range(4):
                act.wait_ge(fold_mm, i + 1)
                nc.scalar.activation(fold_w[:, i].rearrange("p k n -> p (k n)"), fb[i][:, :], ACT.Copy)\
                    .then_inc(fold_ready, 1)
            act.wait_ge(filled, 8)
            act.wait_ge(bd_ready, 1)

            def unpack(n):
                if n < NU:
                    act.wait_ge(code_ready, n + 1)
                    if n >= 2:
                        act.wait_ge(sum6_ready, n - 1)
                    nc.scalar.activation(relu4[:, n % 2], code[:, n % 2], ACT.Relu, bias=act_bias[:, 0:1],
                                         scale=0.125)\
                        .then_inc(relu_ready, 1)
                    if n >= 2:
                        act.wait_ge(deq_ready, n - 1)
                    nc.scalar.activation(relu6[:, n % 2], code[:, n % 2], ACT.Relu, bias=act_bias[:, 1:2],
                                         scale=0.25).then_inc(relu_ready, 1)
                if 1 <= n <= NU:
                    act.wait_ge(deq_ready, n)
                    (m, c), w = units[(n - 1) // 2], (n - 1) % 2
                    nc.scalar.activation(ffn_hi[:, m, w, c * QC:(c + 1) * QC], weight[:, (n - 1) % 2], ACT.Copy)\
                        .then_inc(whi_ready, 1)

            def proj(g, p):
                if p % 2:
                    return
                is_q = p % 4 == 0
                count(act, proj_mm, 8, g, p + 1)
                count(act, qk_ready, 4, g, p // 2 - 1)
                if p < 4:
                    count(act, wo_mm, 2, g, 0)
                nc.scalar.activation(gate_q[:, (p // 2) % 2, :], fb[0][:, :], ACT.Identity,
                                     scale=DK ** -0.5 if is_q else 1.0,
                                     bias=b_small[:, 5:6] if is_q else b_small[:, 3:4]).then_inc(q2_ready, 1)

            def vproj(g, j):
                count(act, v_mm, 2, g, j + 1)
                count(act, o_mm, 16, g, 0)
                nc.scalar.activation(
                    v_sb[:, 2 * j:2 * j + 2].rearrange("p b t (w e) -> p (b t) w e", e=DK)[:, :, 0:3:2, :],
                    fb[2 + j][:, :].rearrange("p (n w e) -> p n w e", w=2, e=DK), ACT.Copy).then_inc(v_ready, 1)

            def square(g, mt):
                count(act, o_mm, 16, g, 8 * mt + 8)
                count(act, qbd_ready, 4, g, 2 * mt + 2)
                nc.scalar.activation(rms_sb[:, mt, :], fb[2 + mt][:, :], ACT.Square).then_inc(sq_ready, 1)

            def rms(g, _):
                count(act, ms_mm, 2, g, 2)
                count(act, rms_ready, 1, g, 1)
                nc.scalar.activation(rms_sb[:].rearrange("p k (n e) -> p (k n) e", e=DK),
                                     inv_rms[:].unsqueeze(2).broadcast_to([P, NB * H, DK]), ACT.Copy)\
                    .then_inc(wide_ready, 1)
                for mt in range(KT):
                    count(act, rT_mm, 2, g, mt + 1)
                    nc.scalar.activation(fac_sb[:, mt, :], fb[mt][:, :], ACT.Copy).then_inc(rT_ready, 1)

            def x1T(g, _):
                for j in range(KT):
                    count(act, x1T_mm, 2, g, j + 1)
                    nc.scalar.activation(x1T_sb[:, j, :], fb[2 + j][:, :], ACT.Copy).then_inc(x1T_ready, 1)

            def finish(g):
                if isinstance(g, int):
                    act.wait_ge(wlo_ready, NU)
                count(act, up_mm, NT, g, 0)
                for w in range(2):
                    count(act, x2T_mm, 2, g, w + 1)
                    nc.scalar.activation(x2T_hi[:, w, :], fb[w][:, :], ACT.Copy).then_inc(x2hi_ready, 1)

            def ffn(g, n):
                count(act, gate_mm, NT, g, n + 1)
                if n:
                    count(act, ilo_ready, NT, g, n)
                nc.scalar.activation(inter[:], gate_ps[:, :], ACT.Gelu_apprx_tanh).then_inc(gelu_ready, 1)
                count(act, inter_ready, NT, g, n + 1)
                if n >= 2:
                    count(act, down_mm, NT, g, n - 1)
                nc.scalar.activation(inter_hi[:, n % 2, :], inter[:], ACT.Copy).then_inc(ihi_ready, 1)

            schedule(act, {"proj": proj, "vproj": vproj, "square": square, "rms": rms, "x1T": x1T}, finish, ffn, lambda g: None, unpack)

        @block.vector
        def _(dve):
            dve.wait_ge(ld_small, 48)
            dve.wait_ge(const_ready, 4)
            for i in range(4):
                nc.vector.tensor_tensor(f_bd[:, i, :].rearrange("p (h e) -> p h e", e=DK), head_one[:],
                                        f_small[:, i, :].unsqueeze(1).broadcast_to([P, HT, DK]), ALU.mult)\
                    .then_inc(dve_const, 1)
            nc.vector.tensor_copy(head_sel[:], head_one[:, :, 0]).then_inc(dve_const, 1)
            nc.vector.tensor_scalar(skip_mat[:], skip_mat[:], skip_sb[:, 0:1], None, ALU.mult).then_inc(dve_const, 1)
            nc.vector.tensor_scalar(b_small[:, 5:6], b_small[:, 1:2], DK ** -0.5, None, ALU.mult).then_inc(bd_ready, 1)
            dve.wait_ge(ld_wo, 32)
            nc.vector.tensor_scalar(wo_sb[:], wo_sb[:], b_small[:, 4:5], None, ALU.mult).then_inc(dve_const, 1)
            dve.wait_ge(dve_const, 7)

            def unpack(n):
                if n < NU:
                    u, w = n // 2, n % 2
                    dve.wait_ge(ld_w[u % 2], 32 * (u // 2 + 1))
                    if n >= 2:
                        dve.wait_ge(relu_ready, 2 * n - 2)
                        dve.wait_ge(deq_ready, n - 1)
                    nc.vector.tensor_scalar(code[:, n % 2], raw_w[:, u % 2], 4 * w, 7, ALU.logical_shift_right,
                                            ALU.bitwise_and).then_inc(code_ready, 1)
                    if n:
                        dve.wait_ge(scale_ready, n)
                    nc.vector.tensor_scalar(sign[:], raw_w[:, u % 2], 4 * w, 8, ALU.logical_shift_right,
                                            ALU.bitwise_and).then_inc(sign_ready, 1)
                    dve.wait_ge(sign_ready, n + 1)
                    nc.vector.scalar_tensor_tensor(sgn_scale[:, n % 2], sign[:], 4.0, raw_s[:, u % 2],
                                                   ALU.subtract, ALU.mult).then_inc(scale_ready, 1)
                if 1 <= n <= NU:
                    q = n - 1
                    dve.wait_ge(relu_ready, 2 * q + 1)
                    nc.vector.scalar_tensor_tensor(relu4[:, q % 2], code[:, q % 2], -0.125, relu4[:, q % 2],
                                                   ALU.mult, ALU.subtract).then_inc(sum4_ready, 1)
                if n >= 2:
                    q = n - 2
                    (m, c), w = units[q // 2], q % 2
                    dve.wait_ge(whi_ready, q + 1)
                    nc.vector.tensor_tensor(ffn_lo[:, m, w, c * QC:(c + 1) * QC], weight[:, q % 2],
                                            ffn_hi[:, m, w, c * QC:(c + 1) * QC].bitcast(F32), ALU.subtract)\
                        .then_inc(wlo_ready, 1)

            def proj(g, p):
                if p % 2 == 0:
                    return
                mt, is_q = p // 4, p % 4 == 1
                count(dve, proj_mm, 8, g, p + 1)
                count(dve, q2_ready, 4, g, p // 2 + 1)
                if is_q:
                    count(dve, on_ready, 2, g, 0)
                else:
                    count(dve, skip_mm, 2, g, 0)
                nc.vector.scalar_tensor_tensor((qT_sb if is_q else kT_sb)[:, mt, :], fb[1][:, :],
                                               b_small[:, 0:1] if is_q else b_small[:, 2:3],
                                               gate_q[:, (p // 2) % 2, :], ALU.add, ALU.mult).then_inc(qk_ready, 1)

            def spread(g, u):
                mt, hc = u // 2, u % 2
                count(dve, qk_ready, 4, g, 2 * mt + 1)
                count(dve, s_mm, 16, g, 4 * u)
                count(dve, y_mm, 16, g, 0)
                count(dve, conv_ready, 16, g, 0)
                for k in range(4):
                    h = 4 * hc + k
                    last = nc.vector.tensor_scalar(qbd[:, k, :], qT_sb[:, mt, :], head_sel[:, h:h + 1], None, ALU.mult)
                last.then_inc(qbd_ready, 1)

            def score(g, u):
                if u == 16:
                    return
                count(dve, s_mm, 16, g, u + 1)
                count(dve, o_mm, 16, g, u - 1)
                nc.vector.tensor_tensor(sc_sb[:, u % 2], fb[u % 2][:, :].rearrange("p (h c) -> p h c", c=P),
                                        causal[:].unsqueeze(1).broadcast_to([P, 4, P]), ALU.mult).then_inc(sm_ready, 1)

            def rms(g, _):
                count(dve, ms_mm, 2, g, 2)
                nc.vector.tensor_scalar(inv_rms[:], fb[0][:, 0:NB * H], 1.0 / DK, RMS_EPS, ALU.mult, ALU.add)\
                    .then_inc(ms_ready, 1)
                count(dve, qk_ready, 4, g, 4)
                for mt in range(KT):
                    count(dve, rT_ready, 2, g, mt + 1)
                    nc.vector.tensor_tensor(o_sb[:, mt, :], fb[2 + mt][:, :], fac_sb[:, mt, :], ALU.mult)\
                        .then_inc(on_ready, 1)

            def stats(g, ln, tile, j):
                for b in (2 * j, 2 * j + 1):
                    if b == 0 and ln < 2:
                        count(dve, ln_ready[ln], NB, g, 0)
                    if b == 2:
                        count(dve, st_ready[ln], NB, g, 2)
                    nc.vector.bn_stats(st[:, ln, b, :], tile[:, b, :]).then_inc(st_ready[ln], 1)
                if j == 0:
                    return
                for b in (0, 1):
                    nc.vector.bn_aggr(mv[:, ln, b, :], st[:, ln, b, :]).then_inc(mv_ready[ln], 1)
                count(dve, st_ready[ln], NB, g, 4)
                count(dve, mv_ready[ln], NB, g, 2)
                nc.vector.tensor_scalar(ve[:, ln, 0:2], mv[:, ln, 0:2, 1], LN_EPS, None, ALU.add).then_inc(ve_ready[ln], 1)
                for b in (2, 3):
                    nc.vector.bn_aggr(mv[:, ln, b, :], st[:, ln, b, :]).then_inc(mv_ready[ln], 1)

            def normalise(g, ln, tile, into):
                count(dve, mv_ready[ln], NB, g, NB)
                nc.vector.tensor_scalar(ve[:, ln, 2:4], mv[:, ln, 2:4, 1], LN_EPS, None, ALU.add).then_inc(ve_ready[ln], 1)
                count(dve, rstd_ready[ln], 1, g, 1)
                for b in range(NB):
                    nc.vector.tensor_scalar(into[:, b, :], tile[:, b, :], mv[:, ln, b, 0:1], ve[:, ln, b:b + 1],
                                            ALU.subtract, ALU.mult).then_inc(ln_ready[ln], 1)

            def outproj(g, j):
                count(dve, wo_mm, 2, g, j + 1)
                count(dve, ld_x, 16, g, 16)
                both = x_sb[:, 2 * j:2 * j + 2].rearrange("p b f -> p (b f)")
                nc.vector.tensor_tensor(both, fb[j][:, :], both, ALU.add).then_inc(y_ready[0], 1)
                count(dve, y_ready[0], 2, g, j + 1)
                stats(g, 0, x_sb, j)
                if j == 1:
                    normalise(g, 0, x_sb, x_sb)

            def conv(g, h):
                count(dve, y_mm, 16, g, h + 1)
                count(dve, ld_ctxT, 16, g, 16)
                if h >= 2:
                    count(dve, conv_ready, 16, g, h - 1)
                for lt in range(KT):
                    c_i = channels(ctxT_sb, lt, h).unsqueeze(2).broadcast_to([P, NB, CI, CI])
                    last = nc.vector.tensor_tensor(pairs(z_sb, h % 2)[:, lt],
                                                   fb[h % 2][:, :].rearrange("p (k b j i) -> p k b j i", k=KT, b=NB, i=CI)[:, lt],
                                                   c_i, ALU.mult)
                last.then_inc(z_ready, 1)
                count(dve, z_ready, 16, g, h + 1)
                nc.vector.tensor_reduce(conv_sb[:, :, :, h * CI:(h + 1) * CI], pairs(z_sb, h % 2), AX.X, ALU.add)\
                    .then_inc(conv_ready, 1)

            def finish(g):
                for j in range(2):
                    both = x_sb[:, 2 * j:2 * j + 2].rearrange("p b f -> p (b f)")
                    ctx2 = ctx_sb[:, 2 * j:2 * j + 2].rearrange("p b f -> p (b f)")
                    count(dve, skip_mm, 2, g, j + 1)
                    nc.vector.tensor_tensor(ctx2, fb[j][:, :], ctx2, ALU.mult).then_inc(sk_ready, 1)
                    count(dve, cT_mm, 2, g, j + 1)
                    nc.vector.tensor_tensor(both, fb[2 + j][:, :], both, ALU.add).then_inc(half_ready, 1)
                    count(dve, half_ready, 2, g, j + 1)
                    count(dve, sk_ready, 2, g, j + 1)
                    nc.vector.tensor_tensor(both, both, ctx2, ALU.add).then_inc(y_ready[1], 1)
                    count(dve, y_ready[1], 2, g, j + 1)
                    stats(g, 1, x_sb, j)
                count(dve, stored, 16, g, 0)
                normalise(g, 1, x_sb, x2_sb)
                for w in range(2):
                    count(dve, x2hi_ready, 2, g, w + 1)
                    nc.vector.tensor_tensor(x2T_lo[:, w, :], fb[w][:, :], x2T_hi[:, w, :].bitcast(F32), ALU.subtract)\
                        .then_inc(x2lo_ready, 1)

            def ffn(g, n):
                count(dve, up_mm, NT, g, n + 1)
                count(dve, gelu_ready, NT, g, n + 1)
                nc.vector.tensor_tensor(inter[:], up_ps[:, :], inter[:], ALU.mult).then_inc(inter_ready, 1)

            def tail(g):
                count(dve, down_mm, NT, g, NT)
                for j in range(2):
                    both = x2_sb[:, 2 * j:2 * j + 2].rearrange("p b f -> p (b f)")
                    nc.vector.tensor_tensor(both, down_ps[j][:, :], both, ALU.add).then_inc(y_ready[2], 1)
                    count(dve, y_ready[2], 2, g, j + 1)
                    stats(g, 2, x2_sb, j)
                normalise(g, 2, x2_sb, x2_sb)

            schedule(dve, {"proj": proj, "qbd": spread, "score": score, "rms": rms, "outproj": outproj, "conv": conv},
                     finish, ffn, tail, unpack)

        @block.tensor
        def _(pe):
            pe.wait_ge(ld_fold, 32)
            pe.wait_ge(dve_const, 7)
            for i in range(4):
                raw = raw_wq if i < 2 else raw_wk
                for kt in range(KT):
                    for mt in range(KT):
                        at = kt * D + mt * P
                        last = nc.tensor.matmul(fb[i][:, at:at + P], raw[:, mt, kt * P:(kt + 1) * P], f_bd[:, i, :],
                                                start=True, stop=True)
                last.then_inc(fold_mm, 1)
            pe.wait_ge(ld_wo, 32)

            def proj(g, p):
                mt, is_k, first = p // 4, p % 4 // 2, p % 2
                if p == 0:
                    count(pe, ld_xT, 16, g, 16)
                    count(pe, x2lo_ready, 2, g, 0)
                    if isinstance(g, int):
                        pe.wait_ge(fold_ready, 4)
                if first:
                    count(pe, qk_ready, 4, g, p // 2)
                else:
                    count(pe, q2_ready, 4, g, p // 2)
                w = fold_w[:, 2 * is_k + (0 if first else 1)]
                for kt in range(KT):
                    last = nc.tensor.matmul(fb[first][:, :], w[:, kt, mt * P:(mt + 1) * P], xT_sb[:, kt, :],
                                            start=kt == 0, stop=kt == KT - 1)
                last.then_inc(proj_mm, 1)

            def vproj(g, j):
                if j == 0:
                    count(pe, half_ready, 2, g, 0)
                for b in (2 * j, 2 * j + 1):
                    for kt in range(KT):
                        last = nc.tensor.matmul(fb[2 + j][:, (b % 2) * D:(b % 2 + 1) * D],
                                                xT_sb[:, kt, b * S:(b + 1) * S], wv_sb[:, kt, :],
                                                start=kt == 0, stop=kt == KT - 1)
                last.then_inc(v_mm, 1)

            def score(g, u):
                if u < 16:
                    mt, hc, b = u // 8, u // 4 % 2, u % 4
                    count(pe, qk_ready, 4, g, 4)
                    count(pe, q2_ready, 4, g, 4)
                    count(pe, qbd_ready, 4, g, 2 * mt + hc + 1)
                    if u >= 2:
                        count(pe, sm_ready, 16, g, u - 1)
                    nc.tensor.matmul(fb[u % 2][:, :].rearrange("p (h c) -> p h c", c=P),
                                     kT_sb[:, mt, b * S:(b + 1) * S], qbd[:, :, b * S:(b + 1) * S],
                                     start=True, stop=True).then_inc(s_mm, 1)
                if u >= 1:
                    u -= 1
                    mt, hc, b = u // 8, u // 4 % 2, u % 4
                    count(pe, v_ready, 2, g, 2)
                    count(pe, sm_ready, 16, g, u + 1)
                    for k in range(4):
                        pair, odd = (4 * hc + k) // 2, k % 2
                        last = nc.tensor.matmul(fb[2 + mt][32 * pair:32 * pair + 32, b * S:(b + 1) * S],
                                                v_sb[:, b, 4 * mt + pair, DK * odd:DK * odd + 2 * DK],
                                                sc_sb[:, u % 2, k, :], start=odd == 0, stop=odd == 1)
                    last.then_inc(o_mm, 1)

            def square(g, mt):
                count(pe, sm_ready, 16, g, 16)
                count(pe, sq_ready, 2, g, mt + 1)
                for b in range(NB):
                    at = b * H + mt * HT
                    last = nc.tensor.matmul(fb[0][:, at:at + HT], rms_sb[:, mt, b * S:(b + 1) * S], head_sel[:],
                                            start=True, stop=True)
                last.then_inc(ms_mm, 1)

            def rms(g, _):
                count(pe, wide_ready, 1, g, 1)
                wide = rms_sb[:].rearrange("p k t -> p (k t)")
                for mt in range(KT):
                    for b in range(NB):
                        at = b * D + mt * P
                        last = nc.tensor.transpose(fb[mt][:, b * S:(b + 1) * S], wide[:, at:at + P], ident[:])
                    last.then_inc(rT_mm, 1)

            def outproj(g, j):
                count(pe, on_ready, 2, g, 2)
                for b in (2 * j, 2 * j + 1):
                    for kt in range(KT):
                        last = nc.tensor.matmul(fb[j][:, (b % 2) * D:(b % 2 + 1) * D],
                                                o_sb[:, kt, b * S:(b + 1) * S], wo_sb[:, kt, :],
                                                start=kt == 0, stop=kt == KT - 1)
                last.then_inc(wo_mm, 1)

            def x1T(g, _):
                count(pe, x1_ready, NB, g, NB)
                for j in range(KT):
                    for b in range(NB):
                        last = nc.tensor.transpose(fb[2 + j][:, b * S:(b + 1) * S], x_sb[:, b, j * P:(j + 1) * P],
                                                   ident[:])
                    last.then_inc(x1T_mm, 1)

            def conv(g, h):
                if h == 0 and isinstance(g, int):
                    pe.wait_ge(ld_toep, 16)
                count(pe, kv_ready, 32, g, 2 * h + 2)
                if h >= 2:
                    count(pe, z_ready, 16, g, h - 1)
                n = NB * CI * CI
                diag, off = toep_sb[:, h, 0:P], toep_sb[:, h, P:2 * P]
                kv = kv_sb[:, h % 2, :]
                nc.tensor.matmul(fb[h % 2][:, 0:n], diag, kv[:, 0:n], start=True, stop=True)
                nc.tensor.matmul(fb[h % 2][:, n:2 * n], off, kv[:, 0:n], start=True, stop=False)
                nc.tensor.matmul(fb[h % 2][:, n:2 * n], diag, kv[:, n:2 * n], start=False, stop=True).then_inc(y_mm, 1)

            def finish(g):
                count(pe, prod_ready, 1, g, 1)
                for j in range(2):
                    count(pe, z_ready, 16, g, 16)
                    nc.tensor.matmul(fb[j][:, :], skip_mat[:].rearrange("p h i -> p (h i)"), prod_sb[:, j, :],
                                     start=True, stop=True).then_inc(skip_mm, 1)
                count(pe, conv_ready, 16, g, 16)
                for j in range(2):
                    for b in (2 * j, 2 * j + 1):
                        for lt in range(KT):
                            at = (b % 2) * D + lt * P
                            last = nc.tensor.transpose(fb[2 + j][:, at:at + P], conv_sb[:, lt, b, :], ident[:])
                    last.then_inc(cT_mm, 1)
                count(pe, x2_ready, NB, g, NB)
                for w in range(2):
                    for b in range(NB):
                        last = nc.tensor.transpose(fb[w][:, b * S:(b + 1) * S], x2_sb[:, b, w::2], ident[:])
                    last.then_inc(x2T_mm, 1)

            def split_mm(ps, w_hi, w_lo, x_hi, x_lo, start, stop):
                nc.tensor.matmul(ps, w_hi, x_lo, start=start, stop=False, skip_group_check=True)
                nc.tensor.matmul(ps, w_lo, x_hi, start=False, stop=False, skip_group_check=True)
                return nc.tensor.matmul(ps, w_hi, x_hi, start=False, stop=stop, skip_group_check=True)

            def down(g, n):
                count(pe, ihi_ready, NT, g, n + 1)
                count(pe, ilo_ready, NT, g, n + 1)
                cols = slice(n // 2 * D, (n // 2 + 1) * D)
                for b in range(NB):
                    toks = slice(b * S, (b + 1) * S)
                    last = split_mm(down_ps[b // 2][:, (b % 2) * D:(b % 2 + 1) * D],
                                    inter_hi[:, n % 2, toks], inter_lo[:, n % 2, toks],
                                    ffn_hi[:, 2, n % 2, cols], ffn_lo[:, 2, n % 2, cols],
                                    n == 0 and b % 2 == 0, n == NT - 1)
                last.then_inc(down_mm, 1)

            def ffn(g, n):
                if n == 0:
                    count(pe, x2hi_ready, 2, g, 2)
                    count(pe, x2lo_ready, 2, g, 2)
                cols = slice(n * P, (n + 1) * P)
                for m, ps, free, done in ((0, gate_ps, gelu_ready, gate_mm), (1, up_ps, inter_ready, up_mm)):
                    if n:
                        count(pe, free, NT, g, n)
                    for w in range(2):
                        last = split_mm(ps[:, :], ffn_hi[:, m, w, cols], ffn_lo[:, m, w, cols],
                                        x2T_hi[:, w, :], x2T_lo[:, w, :], w == 0, w == 1)
                    last.then_inc(done, 1)
                if n >= 1:
                    down(g, n - 1)

            def tail(g):
                down(g, NT - 1)

            schedule(pe, {"proj": proj, "vproj": vproj, "score": score, "square": square, "rms": rms,
                          "outproj": outproj, "x1T": x1T, "conv": conv}, finish, ffn, tail, lambda n: None)


def kernel(**inputs):
    import numpy as np
    import concourse.bacc as bacc
    from concourse.bass_utils import run_bass_kernel_spmd

    a = {name.removeprefix("L0_"): np.asarray(v) for name, v in inputs.items()}
    heads = HT
    taps = a["xattn_k"]
    padded = np.concatenate([np.zeros((CH, P - 1), taps.dtype), taps], axis=1)
    toep = padded[:, P - 1 + np.arange(2 * P)[None, :] - np.arange(P)[:, None]]

    def by_input(packed):
        t = packed.reshape(NT // 2, P, 2, -1).transpose(3, 0, 2, 1)
        return t.reshape(t.shape[0], -1)

    def down_rows(packed):
        t = packed.T.reshape(NT // 2, -1, D).transpose(1, 0, 2)
        return t.reshape(t.shape[0], -1)

    arrays = {
        "x": a["x"],
        "xT": a["x"].transpose(2, 0, 1).reshape(D, B * S),
        "ctx": a["ctx_2048"],
        "ctxT": a["ctx_2048"].transpose(2, 0, 1).reshape(D, B * S),
        "wq": a["attn_wq"],
        "wk": a["attn_wk"],
        "wvT": a["attn_wv"].T,
        "woT": a["attn_wo"].T,
        "fT": np.stack([np.tile(a[f"attn_{n}_w"].T, (heads, 1)) for n in ("fq1", "fq2", "fk1", "fk2")]),
        "bias": np.stack([np.tile(a[n], heads) for n in ("attn_fq1_b", "attn_fq2_b", "attn_fk1_b", "attn_fk2_b",
                                                         "attn_norm_w")], axis=1),
        "skip": a["fside_S2_0"].reshape(P, 1),
        "toep": toep,
        "gate_p": by_input(a["ffn_gate_W_packed"]),
        "gate_s": by_input(a["ffn_gate_scales"]),
        "up_p": by_input(a["ffn_up_W_packed"]),
        "up_s": by_input(a["ffn_up_scales"]),
        "down_p": down_rows(a["ffn_down_W_packed"]),
        "down_s": down_rows(a["ffn_down_scales"]),
    }
    arrays = {n: np.ascontiguousarray(v) for n, v in arrays.items()}
    nc = bacc.Bacc("TRN2", target_bir_lowering=False, num_devices=1)
    aps = {n: nc.dram_tensor(f"in_{n}", v.shape, mybir.dt.from_np(v.dtype), kind="ExternalInput").ap()
           for n, v in arrays.items()}
    out = nc.dram_tensor("out_0", (B, S, D), F32, kind="ExternalOutput").ap()
    decoder_layer(nc, **aps, out=out)
    r = run_bass_kernel_spmd(nc, [{f"in_{n}": v for n, v in arrays.items()}], core_ids=[0])
    return r.results[0]["out_0"]
```

```python
import concourse.bass as bass
from concourse import mybir
from contextlib import ExitStack

F32 = mybir.dt.float32
F32R = mybir.dt.float32r
I32 = mybir.dt.int32
ALU = mybir.AluOpType
ACT = mybir.ActivationFunctionType
AX = mybir.AxisListType

P = 128
B, S, D = 16, 128, 256
H, DK = 16, 16
NB = 4
G = B // NB
T = NB * S
KT = D // P
HT = 8
CH, CI = 16, 8
F = 2048
NT = F // P
QC = 256
NQ = F // QC
LN_EPS = 1e-5
RMS_EPS = 1e-5


def count(eng, sem, per_group, g, k):
    value = per_group * g + k
    if isinstance(value, int) and value <= 0:
        return
    eng.wait_ge(sem, value)


def decoder_layer(nc, x, xT, ctx, ctxT, wq, wk, wvT, woT, fT, bias, skip, toep,
                  gate_p, gate_s, up_p, up_s, down_p, down_s, out):
    x_v = x.rearrange("b t f -> t b f")
    out_v = out.rearrange("b t f -> t b f")
    ctx_v = ctx.rearrange("b t f -> t b f")
    xT_v = xT.rearrange("(k p) t -> p k t", p=P)
    ctxT_v = ctxT.rearrange("(k p) t -> p k t", p=P)

    with ExitStack() as stack:
        def sb(name, shape, dt=F32):
            return stack.enter_context(nc.sbuf_tensor(name, shape, dt))

        def sem(name):
            return stack.enter_context(nc.semaphore(name))

        fold_w = sb("fold_w", [P, 4, KT, D])
        wv_sb = sb("wv_sb", [P, KT, D])
        wo_sb = sb("wo_sb", [P, KT, D])
        ffn_hi = sb("ffn_hi", [P, 3, 2, F], F32R)
        ffn_lo = sb("ffn_lo", [P, 3, 2, F], F32R)
        toep_sb = sb("toep_sb", [P, CH, 2 * P])
        ident = sb("ident", [P, P])
        causal = sb("causal", [P, P])
        head_one = sb("head_one", [P, HT, DK])
        skip_mat = sb("skip_mat", [P, CH, CI])
        head_sel = sb("head_sel", [P, HT])
        f_small = sb("f_small", [P, 4, DK])
        b_small = sb("b_small", [P, 6])
        skip_sb = sb("skip_sb", [P, 1])
        minus_half = sb("minus_half", [P, 1])
        act_bias = sb("act_bias", [P, 2])
        xT_sb = sb("xT_sb", [P, KT, T])
        x1T_sb = sb("x1T_sb", [P, KT, T])
        conv_sb = sb("conv_sb", [P, KT, NB, S])
        x_sb = sb("x_sb", [P, NB, D])
        ctxT_sb = sb("ctxT_sb", [P, KT, T])
        gate_q = sb("gate_q", [P, 2, T])
        o_sb = gate_q
        qT_sb = sb("qT_sb", [P, KT, T])
        rms_sb = qT_sb
        kT_sb = sb("kT_sb", [P, KT, T])
        fac_sb = prod_sb = kT_sb
        sc_sb = sb("sc_sb", [P, 2, 4, P])
        v_sb = sb("v_sb", [P, NB, HT, 3 * DK])
        ctx_sb = sb("ctx_sb", [P, NB, D])
        inv_rms = sb("inv_rms", [P, NB * H])
        ve = sb("ve", [P, 3, NB])
        st = sb("st", [P, 3, NB, 6])
        mv = sb("mv", [P, 3, NB, 2])
        x2_sb = sb("x2_sb", [P, NB, D])
        qbd = sb("qbd", [P, 4, T])
        kv_sb = qbd[:, 0:2, :]
        z_sb = qbd[:, 2:4, :]

        psum = [stack.enter_context(nc.psum_tensor(f"bank{i}", [P, T], F32)) for i in range(8)]
        fb = psum[0:4]
        gate_ps, up_ps = psum[4], psum[5]
        down_ps = psum[6:8]
        skip_ps = x2T_ps = psum[4:6]

        def sems(*names):
            return [sem(n) for n in names]

        ld_fold, ld_wo, ld_toep, ld_small, ld_xT, ld_x, ld_ctxT, ld_ctx, stored = sems(
            "ld_fold", "ld_wo", "ld_toep", "ld_small", "ld_xT", "ld_x", "ld_ctxT", "ld_ctx", "stored")
        ld_w = sems("ld_w_even", "ld_w_odd")
        fold_mm, proj_mm, v_mm, s_mm, o_mm, ms_mm, rT_mm, wo_mm, x1T_mm = sems(
            "fold_mm", "proj_mm", "v_mm", "s_mm", "o_mm", "ms_mm", "rT_mm", "wo_mm", "x1T_mm")
        y_mm, cT_mm, skip_mm, x2T_mm, gate_mm, up_mm, down_mm = sems(
            "y_mm", "cT_mm", "skip_mm", "x2T_mm", "gate_mm", "up_mm", "down_mm")
        fold_ready, q2_ready, v_ready, sq_ready, wide_ready, rT_ready, x1T_ready = sems(
            "fold_ready", "q2_ready", "v_ready", "sq_ready", "wide_ready", "rT_ready", "x1T_ready")
        x2hi_ready, gelu_ready, ihi_ready, relu_ready, whi_ready = sems(
            "x2hi_ready", "gelu_ready", "ihi_ready", "relu_ready", "whi_ready")
        dve_const, bd_ready, qk_ready, qbd_ready, sm_ready, on_ready, z_ready, conv_ready = sems(
            "dve_const", "bd_ready", "qk_ready", "qbd_ready", "sm_ready", "on_ready", "z_ready", "conv_ready")
        ms_ready, half_ready, sk_ready, x2lo_ready, inter_ready, ilo_ready = sems(
            "ms_ready", "half_ready", "sk_ready", "x2lo_ready", "inter_ready", "ilo_ready")
        code_ready, sign_ready, scale_ready, sum4_ready, wlo_ready = sems(
            "code_ready", "sign_ready", "scale_ready", "sum4_ready", "wlo_ready")
        y_ready, st_ready, mv_ready, ve_ready, ln_ready = (
            sems(*[f"{n}{i}" for i in (1, 2, 3)]) for n in ("y_ready", "st_ready", "mv_ready", "ve_ready", "ln_ready"))
        x1_ready, x2_ready, res_ready = ln_ready
        filled, const_ready, pool_mask, rms_ready, kv_ready, prod_ready, sum6_ready, deq_ready = sems(
            "filled", "const_ready", "pool_mask", "rms_ready", "kv_ready", "prod_ready", "sum6_ready", "deq_ready")
        rstd_ready = sems("rstd_ready1", "rstd_ready2", "rstd_ready3")

        with ExitStack() as early:
            def sbe(name, shape, dt=F32):
                return early.enter_context(nc.sbuf_tensor(name, shape, dt))
            raw_w = sbe("raw_w", [P, 2, QC], I32)
            raw_s = sbe("raw_s", [P, 2, QC])
            code = sbe("code", [P, 2, QC], I32)
            sign = sbe("sign", [P, QC], I32)
            sgn_scale = sbe("sgn_scale", [P, 2, QC])
            relu4 = sbe("relu4", [P, 2, QC])
            relu6 = sbe("relu6", [P, 2, QC])
            weight = sbe("weight", [P, 2, QC])
        x2T_hi = sb("x2T_hi", [P, 2, T], F32R)
        x2T_lo = sb("x2T_lo", [P, 2, T], F32R)
        inter = sb("inter", [P, T])
        inter_hi = sb("inter_hi", [P, 2, T], F32R)
        inter_lo = sb("inter_lo", [P, 2, T], F32R)
        raw_q = ctxT_sb
        raw_k = x1T_sb
        f_bd = conv_sb[:].rearrange("p k b s -> p (k b) s")[:, 0:4, :]
        raw_wq = raw_q[:].rearrange("p k (a n) -> p (k a) n", n=D)[:, 0:KT, :]
        raw_wk = raw_k[:].rearrange("p k (a n) -> p (k a) n", n=D)[:, 0:KT, :]

        def channels(tile, kt, h):
            return tile[:, kt, :].rearrange("p (b c) -> p b c", c=S)[:, :, h * CI:(h + 1) * CI]

        def pairs(tile, i):
            return tile[:, i, :].rearrange("p (k b j i) -> p k b j i", k=KT, b=NB, i=CI)

        units = [(m, c) for m in range(3) for c in range(NQ)]
        NU = 2 * len(units)
        UPS = -(-NU // NT)

        packed = [(gate_p, gate_s), (up_p, up_s), (down_p, down_s)]
        scores = [("score", u) for u in range(17)]
        conv = [("conv", h) for h in range(CH)]
        slots = [[] for _ in range(NT)]
        slots[0] = scores[0:4] + [("spread", 1)]
        slots[1] = scores[4:8] + [("spread", 2)]
        slots[2] = scores[8:12] + [("spread", 3)]
        slots[3] = scores[12:17] + [("squares", 0), ("squares", 1)]
        slots[4] = [("sums", 0), ("sums", 1), ("rms", 0)]
        slots[6] = [("wide", 0)]
        slots[7] = [("factor", 0)]
        slots[8] = [("outproj", 0), ("outproj", 1)]
        slots[9] = [("x1T", 0)]
        for n, (h0, h1) in enumerate(((0, 3), (3, 6), (6, 9), (9, 12), (12, 14), (14, 16))):
            slots[10 + n] = conv[h0:h1]

        def run(stages, g, slot):
            for name, k in slots[slot]:
                if name in stages:
                    stages[name](g, k)

        def schedule(eng, turn, front, ffn, tail, unpack):
            turn(None, 0)
            for s in range(NT):
                for n in range(UPS * s, UPS * (s + 1)):
                    unpack(n)
                run(front, 0, s)
            for n in range(UPS * NT, NU + 3):
                unpack(n)
            with eng.Fori(1, G) as g:
                turn(g - 1, g)
                for s in range(NT):
                    ffn(g - 1, s)
                    run(front, g, s)
                tail(g - 1)
            turn(G - 1, None)
            for s in range(NT):
                ffn(G - 1, s)
            tail(G - 1)

        block = stack.enter_context(nc.Block())

        @block.sync
        def _(sp):
            def load(g):
                tok, seq = (g * T, g * NB) if isinstance(g, int) else (sp.snap(g * T), sp.snap(g * NB))
                count(sp, v_mm, 2, g, 0)
                sp.dma_start(xT_sb[:], xT_v[:, :, bass.ds(tok, T)]).then_inc(ld_xT, 16)
                if isinstance(g, int):
                    sp.wait_ge(fold_mm, 4)
                count(sp, z_ready, 16, g, 0)
                sp.dma_start(ctxT_sb[:], ctxT_v[:, :, bass.ds(tok, T)]).then_inc(ld_ctxT, 16)
                count(sp, x2_ready, NB, g, 0)
                sp.dma_start(x_sb[:], x_v[:, bass.ds(seq, NB), :]).then_inc(ld_x, 16)
                sp.dma_start(ctx_sb[:], ctx_v[:, bass.ds(seq, NB), :]).then_inc(ld_ctx, 16)

            sp.dma_start(f_small[:], fT.rearrange("n p e -> p n e")).then_inc(ld_small, 16)
            sp.dma_start(b_small[:, 0:5], bias).then_inc(ld_small, 16)
            sp.dma_start(skip_sb[:], skip).then_inc(ld_small, 16)
            sp.dma_start(raw_wq, wq.rearrange("(k p) n -> p k n", p=P)).then_inc(ld_fold, 16)
            sp.dma_start(raw_wk, wk.rearrange("(k p) n -> p k n", p=P)).then_inc(ld_fold, 16)
            sp.dma_start(wv_sb[:], wvT.rearrange("(k p) n -> p k n", p=P)).then_inc(ld_wo, 16)
            sp.dma_start(wo_sb[:], woT.rearrange("(k p) n -> p k n", p=P)).then_inc(ld_wo, 16)
            load(0)

            def fetch(u):
                m, c = units[u]
                codes, scales = packed[m]
                sp.dma_start(raw_w[:, u % 2, :], codes[:, c * QC:(c + 1) * QC]).then_inc(ld_w[u % 2], 16)
                src = scales[:, c * QC:(c + 1) * QC].unsqueeze(1).broadcast_to([HT, P // HT, QC])
                sp.dma_start(raw_s[:, u % 2, :], src).then_inc(ld_w[u % 2], 16)

            fetch(0)
            fetch(1)
            sp.dma_start(toep_sb[:], toep.rearrange("h p n -> p h n")).then_inc(ld_toep, 16)
            for u in range(2, len(units)):
                sp.wait_ge(scale_ready, 2 * u - 2)
                fetch(u)
            with sp.Fori(1, G) as g:
                load(g)
            sp.wait_ge(stored, 16 * G)

        @block.gpsimd
        def _(pool):
            nc.gpsimd.memset(ident[:], 0.0).then_inc(filled, 1)
            nc.gpsimd.memset(causal[:], 1.0).then_inc(filled, 1)
            nc.gpsimd.memset(head_one[:], 1.0).then_inc(filled, 1)
            nc.gpsimd.memset(skip_mat[:], 1.0).then_inc(filled, 1)
            nc.gpsimd.memset(minus_half[:], -0.5).then_inc(filled, 1)
            nc.gpsimd.memset(v_sb[:], 0.0).then_inc(filled, 1)
            nc.gpsimd.memset(act_bias[:, 0:1], -0.5).then_inc(filled, 1)
            nc.gpsimd.memset(act_bias[:, 1:2], -1.5).then_inc(filled, 1)
            pool.wait_ge(filled, 8)
            masks = ((head_one, HT, DK), (skip_mat, CH, CI))
            for tile, n, w in masks:
                nc.gpsimd.affine_select(out=tile[:], in_=tile[:], compare_op=ALU.is_ge, fill=0.0, base=0,
                                        pattern=[[-w, n], [0, w]], channel_multiplier=1).then_inc(pool_mask, 1)
            pool.wait_ge(pool_mask, 2)
            for tile, n, w in masks:
                nc.gpsimd.affine_select(out=tile[:], in_=tile[:], compare_op=ALU.is_ge, fill=0.0, base=w - 1,
                                        pattern=[[w, n], [0, w]], channel_multiplier=-1).then_inc(const_ready, 1)
            nc.gpsimd.affine_select(out=ident[:], in_=ident[:], compare_op=ALU.not_equal, fill=1.0,
                                    base=0, pattern=[[-1, P]], channel_multiplier=1).then_inc(const_ready, 1)
            nc.gpsimd.affine_select(out=causal[:], in_=causal[:], compare_op=ALU.is_ge, fill=0.0,
                                    base=0, pattern=[[1, P]], channel_multiplier=-1).then_inc(const_ready, 1)

            def unpack(step):
                n = step - 1
                if n < 0 or n >= NU:
                    return
                pool.wait_ge(relu_ready, 2 * n + 2)
                pool.wait_ge(sum4_ready, n + 1)
                nc.gpsimd.tensor_tensor(relu6[:, n % 2], relu4[:, n % 2], relu6[:, n % 2], ALU.subtract)\
                    .then_inc(sum6_ready, 1)
                pool.wait_ge(sum6_ready, n + 1)
                pool.wait_ge(scale_ready, n + 1)
                if n >= 2:
                    pool.wait_ge(whi_ready, n - 1)
                    pool.wait_ge(wlo_ready, n - 1)
                nc.gpsimd.tensor_tensor(weight[:, n % 2], relu6[:, n % 2], sgn_scale[:, n % 2], ALU.mult)\
                    .then_inc(deq_ready, 1)

            def rms(g, _):
                count(pool, ms_ready, 1, g, 1)
                nc.gpsimd.tensor_tensor(inv_rms[:], inv_rms[:], minus_half[:].broadcast_to([P, NB * H]),
                                        ALU.pow).then_inc(rms_ready, 1)

            def rstd(g, ln):
                count(pool, ve_ready[ln], 2, g, 2)
                nc.gpsimd.tensor_tensor(ve[:, ln, :], ve[:, ln, :], minus_half[:].broadcast_to([P, NB]),
                                        ALU.pow).then_inc(rstd_ready[ln], 1)

            def outproj(g, j):
                if j == 1:
                    rstd(g, 0)

            def x1T(g, _):
                count(pool, x1_ready, NB, g, NB)
                count(pool, ld_ctx, 16, g, 16)
                count(pool, s_mm, 16, g, 16)
                nc.gpsimd.tensor_tensor(prod_sb[:].rearrange("p k t -> p (k t)"),
                                        x_sb[:].rearrange("p b f -> p (b f)"),
                                        ctx_sb[:].rearrange("p b f -> p (b f)"), ALU.mult).then_inc(prod_ready, 1)

            def conv(g, h):
                if h == 0:
                    count(pool, ld_ctxT, 16, g, 16)
                    count(pool, x1T_ready, 2, g, 2)
                    count(pool, s_mm, 16, g, 16)
                if h >= 2:
                    count(pool, y_mm, 16, g, h - 1)
                for kt in range(KT):
                    v_i = channels(x1T_sb, kt, h).unsqueeze(2).broadcast_to([P, NB, CI, CI])
                    c_j = channels(ctxT_sb, kt, h).unsqueeze(3).broadcast_to([P, NB, CI, CI])
                    nc.gpsimd.tensor_tensor(pairs(kv_sb, h % 2)[:, kt], v_i, c_j, ALU.mult).then_inc(kv_ready, 1)

            def turn(prev, _):
                if prev is not None:
                    rstd(prev, 1)

            def tail(g):
                rstd(g, 2)
                at = g * NB if isinstance(g, int) else pool.snap(g * NB)
                count(pool, res_ready, NB, g, NB)
                pool.dma_start(out_v[:, bass.ds(at, NB), :], x2_sb[:]).then_inc(stored, 16)
                count(pool, stored, 16, g, 16)

            schedule(pool, turn, {"rms": rms, "outproj": outproj, "x1T": x1T, "conv": conv}, lambda g, n: None, tail,
                     unpack)

        @block.scalar
        def _(act):
            for i in range(4):
                act.wait_ge(fold_mm, i + 1)
                nc.scalar.activation(fold_w[:, i].rearrange("p k n -> p (k n)"), fb[i][:, :], ACT.Copy)\
                    .then_inc(fold_ready, 1)
            act.wait_ge(filled, 8)
            act.wait_ge(bd_ready, 1)

            def unpack(n):
                if n < NU:
                    act.wait_ge(code_ready, n + 1)
                    if n >= 2:
                        act.wait_ge(sum6_ready, n - 1)
                    nc.scalar.activation(relu4[:, n % 2], code[:, n % 2], ACT.Relu, bias=act_bias[:, 0:1],
                                         scale=0.125)\
                        .then_inc(relu_ready, 1)
                    if n >= 2:
                        act.wait_ge(deq_ready, n - 1)
                    nc.scalar.activation(relu6[:, n % 2], code[:, n % 2], ACT.Relu, bias=act_bias[:, 1:2],
                                         scale=0.25).then_inc(relu_ready, 1)
                if 2 <= n <= NU + 1:
                    q = n - 2
                    act.wait_ge(deq_ready, q + 1)
                    (m, c), w = units[q // 2], q % 2
                    nc.scalar.activation(ffn_hi[:, m, w, c * QC:(c + 1) * QC], weight[:, q % 2], ACT.Copy)\
                        .then_inc(whi_ready, 1)

            def proj(g, p):
                if p % 2:
                    return
                is_q = p % 4 == 0
                count(act, proj_mm, 8, g, p + 1)
                count(act, qk_ready, 4, g, p // 2 - 1)
                if p < 4:
                    count(act, wo_mm, 2, g, 0)
                nc.scalar.activation(gate_q[:, (p // 2) % 2, :], fb[0][:, :], ACT.Identity,
                                     scale=DK ** -0.5 if is_q else 1.0,
                                     bias=b_small[:, 5:6] if is_q else b_small[:, 3:4]).then_inc(q2_ready, 1)

            def vproj(g, j):
                count(act, v_mm, 2, g, j + 1)
                count(act, o_mm, 16, g, 0)
                nc.scalar.activation(
                    v_sb[:, 2 * j:2 * j + 2].rearrange("p b t (w e) -> p (b t) w e", e=DK)[:, :, 0:3:2, :],
                    fb[2 + j][:, :].rearrange("p (n w e) -> p n w e", w=2, e=DK), ACT.Copy).then_inc(v_ready, 1)

            def spread(g, u):
                mt, hc = u // 2, u % 2
                count(act, qk_ready, 4, g, 2 * mt + 1)
                count(act, s_mm, 16, g, 4 * u)
                if u == 0:
                    count(act, y_mm, 16, g, 0)
                    count(act, conv_ready, 16, g, 0)
                for k in range(4):
                    h = 4 * hc + k
                    last = nc.scalar.activation(qbd[:, k, :], qT_sb[:, mt, :], ACT.Copy, scale=head_sel[:, h:h + 1])
                last.then_inc(qbd_ready, 1)

            def squares(g, mt):
                count(act, o_mm, 16, g, 8 * mt + 8)
                count(act, qbd_ready, 4, g, 2 * mt + 2)
                nc.scalar.activation(rms_sb[:, mt, :], fb[2 + mt][:, :], ACT.Square).then_inc(sq_ready, 1)

            def wide(g, _):
                count(act, ms_mm, 2, g, 2)
                count(act, rms_ready, 1, g, 1)
                nc.scalar.activation(rms_sb[:].rearrange("p k (n e) -> p (k n) e", e=DK),
                                     inv_rms[:].unsqueeze(2).broadcast_to([P, NB * H, DK]), ACT.Copy)\
                    .then_inc(wide_ready, 1)

            def factor(g, _):
                for mt in range(KT):
                    count(act, rT_mm, 2, g, mt + 1)
                    nc.scalar.activation(fac_sb[:, mt, :], fb[mt][:, :], ACT.Copy).then_inc(rT_ready, 1)

            def x1T(g, _):
                for j in range(KT):
                    count(act, x1T_mm, 2, g, j + 1)
                    nc.scalar.activation(x1T_sb[:, j, :], fb[2 + j][:, :], ACT.Copy).then_inc(x1T_ready, 1)

            def turn(prev, g):
                if g is not None:
                    for p in range(8):
                        proj(g, p)
                    spread(g, 0)
                    vproj(g, 0)
                if prev is not None:
                    if isinstance(prev, int):
                        act.wait_ge(wlo_ready, NU)
                    for w in range(2):
                        count(act, x2T_mm, 2, prev, w + 1)
                        nc.scalar.activation(x2T_hi[:, w, :], x2T_ps[w][:, :], ACT.Copy).then_inc(x2hi_ready, 1)
                if g is not None:
                    vproj(g, 1)

            def ffn(g, n):
                count(act, gate_mm, NT, g, n + 1)
                if n:
                    count(act, ilo_ready, NT, g, n)
                nc.scalar.activation(inter[:], gate_ps[:, :], ACT.Gelu_apprx_tanh).then_inc(gelu_ready, 1)
                count(act, inter_ready, NT, g, n + 1)
                if n >= 2:
                    count(act, down_mm, NT, g, n - 1)
                nc.scalar.activation(inter_hi[:, n % 2, :], inter[:], ACT.Copy).then_inc(ihi_ready, 1)

            schedule(act, turn, {"spread": spread, "squares": squares, "wide": wide, "factor": factor, "x1T": x1T},
                     ffn, lambda g: None, unpack)

        @block.vector
        def _(dve):
            dve.wait_ge(ld_small, 48)
            dve.wait_ge(const_ready, 4)
            for i in range(4):
                nc.vector.tensor_tensor(f_bd[:, i, :].rearrange("p (h e) -> p h e", e=DK), head_one[:],
                                        f_small[:, i, :].unsqueeze(1).broadcast_to([P, HT, DK]), ALU.mult)\
                    .then_inc(dve_const, 1)
            nc.vector.tensor_copy(head_sel[:], head_one[:, :, 0]).then_inc(dve_const, 1)
            nc.vector.tensor_scalar(skip_mat[:], skip_mat[:], skip_sb[:, 0:1], None, ALU.mult).then_inc(dve_const, 1)
            nc.vector.tensor_scalar(b_small[:, 5:6], b_small[:, 1:2], DK ** -0.5, None, ALU.mult).then_inc(bd_ready, 1)
            dve.wait_ge(ld_wo, 32)
            nc.vector.tensor_scalar(wo_sb[:], wo_sb[:], b_small[:, 4:5], None, ALU.mult).then_inc(dve_const, 1)
            dve.wait_ge(dve_const, 7)

            def unpack(n):
                if n < NU:
                    u, w = n // 2, n % 2
                    dve.wait_ge(ld_w[u % 2], 32 * (u // 2 + 1))
                    if n >= 2:
                        dve.wait_ge(relu_ready, 2 * n - 2)
                        dve.wait_ge(deq_ready, n - 1)
                    nc.vector.tensor_scalar(code[:, n % 2], raw_w[:, u % 2], 4 * w, 7, ALU.logical_shift_right,
                                            ALU.bitwise_and).then_inc(code_ready, 1)
                    if n:
                        dve.wait_ge(scale_ready, n)
                    nc.vector.tensor_scalar(sign[:], raw_w[:, u % 2], 4 * w, 8, ALU.logical_shift_right,
                                            ALU.bitwise_and).then_inc(sign_ready, 1)
                    dve.wait_ge(sign_ready, n + 1)
                    nc.vector.scalar_tensor_tensor(sgn_scale[:, n % 2], sign[:], 4.0, raw_s[:, u % 2],
                                                   ALU.subtract, ALU.mult).then_inc(scale_ready, 1)
                if 1 <= n <= NU:
                    q = n - 1
                    dve.wait_ge(relu_ready, 2 * q + 1)
                    nc.vector.scalar_tensor_tensor(relu4[:, q % 2], code[:, q % 2], -0.125, relu4[:, q % 2],
                                                   ALU.mult, ALU.subtract).then_inc(sum4_ready, 1)
                if n >= 3:
                    q = n - 3
                    (m, c), w = units[q // 2], q % 2
                    dve.wait_ge(whi_ready, q + 1)
                    nc.vector.tensor_tensor(ffn_lo[:, m, w, c * QC:(c + 1) * QC], weight[:, q % 2],
                                            ffn_hi[:, m, w, c * QC:(c + 1) * QC].bitcast(F32), ALU.subtract)\
                        .then_inc(wlo_ready, 1)

            def proj(g, p):
                if p % 2 == 0:
                    return
                mt, is_q = p // 4, p % 4 == 1
                count(dve, proj_mm, 8, g, p + 1)
                count(dve, q2_ready, 4, g, p // 2 + 1)
                if is_q:
                    count(dve, on_ready, 2, g, 0)
                else:
                    count(dve, skip_mm, 2, g, 0)
                nc.vector.scalar_tensor_tensor((qT_sb if is_q else kT_sb)[:, mt, :], fb[1][:, :],
                                               b_small[:, 0:1] if is_q else b_small[:, 2:3],
                                               gate_q[:, (p // 2) % 2, :], ALU.add, ALU.mult).then_inc(qk_ready, 1)

            def score(g, u):
                if u == 16:
                    return
                count(dve, s_mm, 16, g, u + 1)
                count(dve, o_mm, 16, g, u - 1)
                nc.vector.tensor_tensor(sc_sb[:, u % 2], fb[u % 2][:, :].rearrange("p (h c) -> p h c", c=P),
                                        causal[:].unsqueeze(1).broadcast_to([P, 4, P]), ALU.mult).then_inc(sm_ready, 1)

            def rms(g, _):
                count(dve, ms_mm, 2, g, 2)
                nc.vector.tensor_scalar(inv_rms[:], fb[0][:, 0:NB * H], 1.0 / DK, RMS_EPS, ALU.mult, ALU.add)\
                    .then_inc(ms_ready, 1)

            def factor(g, _):
                count(dve, qk_ready, 4, g, 4)
                for mt in range(KT):
                    count(dve, rT_ready, 2, g, mt + 1)
                    nc.vector.tensor_tensor(o_sb[:, mt, :], fb[2 + mt][:, :], fac_sb[:, mt, :], ALU.mult)\
                        .then_inc(on_ready, 1)

            def stats(g, ln, tile, j):
                for b in (2 * j, 2 * j + 1):
                    if b == 2:
                        count(dve, st_ready[ln], NB, g, 2)
                    nc.vector.bn_stats(st[:, ln, b, :], tile[:, b, :]).then_inc(st_ready[ln], 1)
                if j == 0:
                    return
                for b in (0, 1):
                    nc.vector.bn_aggr(mv[:, ln, b, :], st[:, ln, b, :]).then_inc(mv_ready[ln], 1)
                count(dve, st_ready[ln], NB, g, 4)
                count(dve, mv_ready[ln], NB, g, 2)
                nc.vector.tensor_scalar(ve[:, ln, 0:2], mv[:, ln, 0:2, 1], LN_EPS, None, ALU.add).then_inc(ve_ready[ln], 1)
                for b in (2, 3):
                    nc.vector.bn_aggr(mv[:, ln, b, :], st[:, ln, b, :]).then_inc(mv_ready[ln], 1)

            def normalise(g, ln, tile, into):
                count(dve, mv_ready[ln], NB, g, NB)
                nc.vector.tensor_scalar(ve[:, ln, 2:4], mv[:, ln, 2:4, 1], LN_EPS, None, ALU.add).then_inc(ve_ready[ln], 1)
                count(dve, rstd_ready[ln], 1, g, 1)
                for b in range(NB):
                    nc.vector.tensor_scalar(into[:, b, :], tile[:, b, :], mv[:, ln, b, 0:1], ve[:, ln, b:b + 1],
                                            ALU.subtract, ALU.mult).then_inc(ln_ready[ln], 1)

            def outproj(g, j):
                count(dve, wo_mm, 2, g, j + 1)
                count(dve, ld_x, 16, g, 16)
                both = x_sb[:, 2 * j:2 * j + 2].rearrange("p b f -> p (b f)")
                nc.vector.tensor_tensor(both, fb[j][:, :], both, ALU.add).then_inc(y_ready[0], 1)
                count(dve, y_ready[0], 2, g, j + 1)
                stats(g, 0, x_sb, j)
                if j == 1:
                    normalise(g, 0, x_sb, x_sb)

            def conv(g, h):
                count(dve, y_mm, 16, g, h + 1)
                count(dve, ld_ctxT, 16, g, 16)
                if h >= 2:
                    count(dve, conv_ready, 16, g, h - 1)
                for lt in range(KT):
                    c_i = channels(ctxT_sb, lt, h).unsqueeze(2).broadcast_to([P, NB, CI, CI])
                    last = nc.vector.tensor_tensor(pairs(z_sb, h % 2)[:, lt],
                                                   fb[h % 2][:, :].rearrange("p (k b j i) -> p k b j i", k=KT, b=NB, i=CI)[:, lt],
                                                   c_i, ALU.mult)
                last.then_inc(z_ready, 1)
                count(dve, z_ready, 16, g, h + 1)
                nc.vector.tensor_reduce(conv_sb[:, :, :, h * CI:(h + 1) * CI], pairs(z_sb, h % 2), AX.X, ALU.add)\
                    .then_inc(conv_ready, 1)

            def x2_half(g, j):
                both = x_sb[:, 2 * j:2 * j + 2].rearrange("p b f -> p (b f)")
                ctx2 = ctx_sb[:, 2 * j:2 * j + 2].rearrange("p b f -> p (b f)")
                count(dve, skip_mm, 2, g, j + 1)
                nc.vector.tensor_tensor(ctx2, skip_ps[j][:, :], ctx2, ALU.mult).then_inc(sk_ready, 1)
                count(dve, cT_mm, 2, g, j + 1)
                nc.vector.tensor_tensor(both, fb[2 + j][:, :], both, ALU.add).then_inc(half_ready, 1)
                count(dve, half_ready, 2, g, j + 1)
                count(dve, sk_ready, 2, g, j + 1)
                nc.vector.tensor_tensor(both, both, ctx2, ALU.add).then_inc(y_ready[1], 1)
                count(dve, y_ready[1], 2, g, j + 1)
                stats(g, 1, x_sb, j)

            def turn(prev, g):
                if prev is not None:
                    x2_half(prev, 0)
                if g is not None:
                    proj(g, 1)
                if prev is not None:
                    x2_half(prev, 1)
                if g is not None:
                    proj(g, 3)
                if prev is not None:
                    normalise(prev, 1, x_sb, x2_sb)
                if g is not None:
                    proj(g, 5)
                    proj(g, 7)
                if prev is not None:
                    for w in range(2):
                        count(dve, x2hi_ready, 2, prev, w + 1)
                        nc.vector.tensor_tensor(x2T_lo[:, w, :], x2T_ps[w][:, :], x2T_hi[:, w, :].bitcast(F32),
                                                ALU.subtract).then_inc(x2lo_ready, 1)

            def split(g, n):
                count(dve, ihi_ready, NT, g, n + 1)
                if n >= 2:
                    count(dve, down_mm, NT, g, n - 1)
                nc.vector.tensor_tensor(inter_lo[:, n % 2, :], inter[:], inter_hi[:, n % 2, :].bitcast(F32),
                                        ALU.subtract).then_inc(ilo_ready, 1)

            def ffn(g, n):
                if n:
                    split(g, n - 1)
                count(dve, up_mm, NT, g, n + 1)
                count(dve, gelu_ready, NT, g, n + 1)
                nc.vector.tensor_tensor(inter[:], up_ps[:, :], inter[:], ALU.mult).then_inc(inter_ready, 1)

            def tail(g):
                split(g, NT - 1)
                count(dve, down_mm, NT, g, NT)
                for j in range(2):
                    both = x2_sb[:, 2 * j:2 * j + 2].rearrange("p b f -> p (b f)")
                    nc.vector.tensor_tensor(both, down_ps[j][:, :], both, ALU.add).then_inc(y_ready[2], 1)
                    count(dve, y_ready[2], 2, g, j + 1)
                    stats(g, 2, x2_sb, j)
                normalise(g, 2, x2_sb, x2_sb)

            schedule(dve, turn, {"score": score, "rms": rms, "factor": factor, "outproj": outproj, "conv": conv}, ffn,
                     tail, unpack)

        @block.tensor
        def _(pe):
            pe.wait_ge(ld_fold, 32)
            pe.wait_ge(dve_const, 7)
            for i in range(4):
                raw = raw_wq if i < 2 else raw_wk
                for kt in range(KT):
                    for mt in range(KT):
                        at = kt * D + mt * P
                        last = nc.tensor.matmul(fb[i][:, at:at + P], raw[:, mt, kt * P:(kt + 1) * P], f_bd[:, i, :],
                                                start=True, stop=True)
                last.then_inc(fold_mm, 1)
            pe.wait_ge(ld_wo, 32)

            def proj(g, p):
                mt, is_k, first = p // 4, p % 4 // 2, p % 2
                if p == 0:
                    count(pe, ld_xT, 16, g, 16)
                    count(pe, z_ready, 16, g, 0)
                    if isinstance(g, int):
                        pe.wait_ge(fold_ready, 4)
                if first:
                    count(pe, qk_ready, 4, g, p // 2)
                else:
                    count(pe, q2_ready, 4, g, p // 2)
                w = fold_w[:, 2 * is_k + (0 if first else 1)]
                for kt in range(KT):
                    last = nc.tensor.matmul(fb[first][:, :], w[:, kt, mt * P:(mt + 1) * P], xT_sb[:, kt, :],
                                            start=kt == 0, stop=kt == KT - 1)
                last.then_inc(proj_mm, 1)

            def vproj(g, j):
                if j == 0:
                    count(pe, half_ready, 2, g, 0)
                for b in (2 * j, 2 * j + 1):
                    for kt in range(KT):
                        last = nc.tensor.matmul(fb[2 + j][:, (b % 2) * D:(b % 2 + 1) * D],
                                                xT_sb[:, kt, b * S:(b + 1) * S], wv_sb[:, kt, :],
                                                start=kt == 0, stop=kt == KT - 1)
                last.then_inc(v_mm, 1)

            def score(g, u):
                if u < 16:
                    mt, hc, b = u // 8, u // 4 % 2, u % 4
                    count(pe, qk_ready, 4, g, 4)
                    count(pe, q2_ready, 4, g, 4)
                    count(pe, qbd_ready, 4, g, 2 * mt + hc + 1)
                    if u >= 2:
                        count(pe, sm_ready, 16, g, u - 1)
                    nc.tensor.matmul(fb[u % 2][:, :].rearrange("p (h c) -> p h c", c=P),
                                     kT_sb[:, mt, b * S:(b + 1) * S], qbd[:, :, b * S:(b + 1) * S],
                                     start=True, stop=True).then_inc(s_mm, 1)
                if u >= 1:
                    u -= 1
                    mt, hc, b = u // 8, u // 4 % 2, u % 4
                    count(pe, v_ready, 2, g, 2)
                    count(pe, sm_ready, 16, g, u + 1)
                    for k in range(4):
                        pair, odd = (4 * hc + k) // 2, k % 2
                        last = nc.tensor.matmul(fb[2 + mt][32 * pair:32 * pair + 32, b * S:(b + 1) * S],
                                                v_sb[:, b, 4 * mt + pair, DK * odd:DK * odd + 2 * DK],
                                                sc_sb[:, u % 2, k, :], start=odd == 0, stop=odd == 1)
                    last.then_inc(o_mm, 1)

            def sums(g, mt):
                count(pe, sm_ready, 16, g, 16)
                count(pe, sq_ready, 2, g, mt + 1)
                for b in range(NB):
                    at = b * H + mt * HT
                    last = nc.tensor.matmul(fb[0][:, at:at + HT], rms_sb[:, mt, b * S:(b + 1) * S], head_sel[:],
                                            start=True, stop=True)
                last.then_inc(ms_mm, 1)

            def factor(g, _):
                count(pe, wide_ready, 1, g, 1)
                wide = rms_sb[:].rearrange("p k t -> p (k t)")
                for mt in range(KT):
                    for b in range(NB):
                        at = b * D + mt * P
                        last = nc.tensor.transpose(fb[mt][:, b * S:(b + 1) * S], wide[:, at:at + P], ident[:])
                    last.then_inc(rT_mm, 1)

            def outproj(g, j):
                count(pe, on_ready, 2, g, 2)
                for b in (2 * j, 2 * j + 1):
                    for kt in range(KT):
                        last = nc.tensor.matmul(fb[j][:, (b % 2) * D:(b % 2 + 1) * D],
                                                o_sb[:, kt, b * S:(b + 1) * S], wo_sb[:, kt, :],
                                                start=kt == 0, stop=kt == KT - 1)
                last.then_inc(wo_mm, 1)

            def x1T(g, _):
                count(pe, x1_ready, NB, g, NB)
                for j in range(KT):
                    for b in range(NB):
                        last = nc.tensor.transpose(fb[2 + j][:, b * S:(b + 1) * S], x_sb[:, b, j * P:(j + 1) * P],
                                                   ident[:])
                    last.then_inc(x1T_mm, 1)

            def conv(g, h):
                if h == 0 and isinstance(g, int):
                    pe.wait_ge(ld_toep, 16)
                count(pe, kv_ready, 32, g, 2 * h + 2)
                if h >= 2:
                    count(pe, z_ready, 16, g, h - 1)
                n = NB * CI * CI
                diag, off = toep_sb[:, h, 0:P], toep_sb[:, h, P:2 * P]
                kv = kv_sb[:, h % 2, :]
                nc.tensor.matmul(fb[h % 2][:, 0:n], diag, kv[:, 0:n], start=True, stop=True)
                nc.tensor.matmul(fb[h % 2][:, n:2 * n], off, kv[:, 0:n], start=True, stop=False)
                nc.tensor.matmul(fb[h % 2][:, n:2 * n], diag, kv[:, n:2 * n], start=False, stop=True).then_inc(y_mm, 1)

            def conv_out(g):
                count(pe, prod_ready, 1, g, 1)
                for j in range(2):
                    nc.tensor.matmul(skip_ps[j][:, :], skip_mat[:].rearrange("p h i -> p (h i)"), prod_sb[:, j, :],
                                     start=True, stop=True).then_inc(skip_mm, 1)
                count(pe, conv_ready, 16, g, 16)
                for j in range(2):
                    for b in (2 * j, 2 * j + 1):
                        for lt in range(KT):
                            at = (b % 2) * D + lt * P
                            last = nc.tensor.transpose(fb[2 + j][:, at:at + P], conv_sb[:, lt, b, :], ident[:])
                    last.then_inc(cT_mm, 1)

            def x2T(g):
                count(pe, sk_ready, 2, g, 2)
                count(pe, x2_ready, NB, g, NB)
                for w in range(2):
                    for b in range(NB):
                        last = nc.tensor.transpose(x2T_ps[w][:, b * S:(b + 1) * S], x2_sb[:, b, w::2], ident[:])
                    last.then_inc(x2T_mm, 1)

            def turn(prev, g):
                if prev is not None:
                    conv_out(prev)
                if g is not None:
                    for p in range(8):
                        proj(g, p)
                    vproj(g, 0)
                if prev is not None:
                    x2T(prev)
                if g is not None:
                    vproj(g, 1)

            def split_mm(ps, w_hi, w_lo, x_hi, x_lo, start, stop):
                nc.tensor.matmul(ps, w_hi, x_lo, start=start, stop=False, skip_group_check=True)
                nc.tensor.matmul(ps, w_lo, x_hi, start=False, stop=False, skip_group_check=True)
                return nc.tensor.matmul(ps, w_hi, x_hi, start=False, stop=stop, skip_group_check=True)

            def down(g, n):
                count(pe, ihi_ready, NT, g, n + 1)
                count(pe, ilo_ready, NT, g, n + 1)
                cols = slice(n // 2 * D, (n // 2 + 1) * D)
                for b in range(NB):
                    toks = slice(b * S, (b + 1) * S)
                    last = split_mm(down_ps[b // 2][:, (b % 2) * D:(b % 2 + 1) * D],
                                    inter_hi[:, n % 2, toks], inter_lo[:, n % 2, toks],
                                    ffn_hi[:, 2, n % 2, cols], ffn_lo[:, 2, n % 2, cols],
                                    n == 0 and b % 2 == 0, n == NT - 1)
                last.then_inc(down_mm, 1)

            def ffn(g, n):
                if n == 0:
                    count(pe, x2hi_ready, 2, g, 2)
                    count(pe, x2lo_ready, 2, g, 2)
                cols = slice(n * P, (n + 1) * P)
                for m, ps, free, done in ((0, gate_ps, gelu_ready, gate_mm), (1, up_ps, inter_ready, up_mm)):
                    if n:
                        count(pe, free, NT, g, n)
                    for w in range(2):
                        last = split_mm(ps[:, :], ffn_hi[:, m, w, cols], ffn_lo[:, m, w, cols],
                                        x2T_hi[:, w, :], x2T_lo[:, w, :], w == 0, w == 1)
                    last.then_inc(done, 1)
                if n >= 1:
                    down(g, n - 1)

            def tail(g):
                down(g, NT - 1)

            schedule(pe, turn, {"score": score, "sums": sums, "factor": factor, "outproj": outproj, "x1T": x1T,
                                "conv": conv}, ffn, tail, lambda n: None)


def kernel(**inputs):
    import numpy as np
    import concourse.bacc as bacc
    from concourse.bass_utils import run_bass_kernel_spmd

    a = {name.removeprefix("L0_"): np.asarray(v) for name, v in inputs.items()}
    heads = HT
    taps = a["xattn_k"]
    padded = np.concatenate([np.zeros((CH, P - 1), taps.dtype), taps], axis=1)
    toep = padded[:, P - 1 + np.arange(2 * P)[None, :] - np.arange(P)[:, None]]

    def by_input(packed):
        t = packed.reshape(NT // 2, P, 2, -1).transpose(3, 0, 2, 1)
        return t.reshape(t.shape[0], -1)

    def down_rows(packed):
        t = packed.T.reshape(NT // 2, -1, D).transpose(1, 0, 2)
        return t.reshape(t.shape[0], -1)

    arrays = {
        "x": a["x"],
        "xT": a["x"].transpose(2, 0, 1).reshape(D, B * S),
        "ctx": a["ctx_2048"],
        "ctxT": a["ctx_2048"].transpose(2, 0, 1).reshape(D, B * S),
        "wq": a["attn_wq"],
        "wk": a["attn_wk"],
        "wvT": a["attn_wv"].T,
        "woT": a["attn_wo"].T,
        "fT": np.stack([np.tile(a[f"attn_{n}_w"].T, (heads, 1)) for n in ("fq1", "fq2", "fk1", "fk2")]),
        "bias": np.stack([np.tile(a[n], heads) for n in ("attn_fq1_b", "attn_fq2_b", "attn_fk1_b", "attn_fk2_b",
                                                         "attn_norm_w")], axis=1),
        "skip": a["fside_S2_0"].reshape(P, 1),
        "toep": toep,
        "gate_p": by_input(a["ffn_gate_W_packed"]),
        "gate_s": by_input(a["ffn_gate_scales"]),
        "up_p": by_input(a["ffn_up_W_packed"]),
        "up_s": by_input(a["ffn_up_scales"]),
        "down_p": down_rows(a["ffn_down_W_packed"]),
        "down_s": down_rows(a["ffn_down_scales"]),
    }
    arrays = {n: np.ascontiguousarray(v) for n, v in arrays.items()}
    nc = bacc.Bacc("TRN2", target_bir_lowering=False, num_devices=1)
    aps = {n: nc.dram_tensor(f"in_{n}", v.shape, mybir.dt.from_np(v.dtype), kind="ExternalInput").ap()
           for n, v in arrays.items()}
    out = nc.dram_tensor("out_0", (B, S, D), F32, kind="ExternalOutput").ap()
    decoder_layer(nc, **aps, out=out)
    r = run_bass_kernel_spmd(nc, [{f"in_{n}": v for n, v in arrays.items()}], core_ids=[0])
    return r.results[0]["out_0"]
```

```python
import concourse.bass as bass
from concourse import mybir
from contextlib import ExitStack

F32 = mybir.dt.float32
F32R = mybir.dt.float32r
I32 = mybir.dt.int32
ALU = mybir.AluOpType
ACT = mybir.ActivationFunctionType
AX = mybir.AxisListType

P = 128
B, S, D = 16, 128, 256
H, DK = 16, 16
NB = 4
G = B // NB
T = NB * S
KT = D // P
HT = 8
CH, CI = 16, 8
F = 2048
NT = F // P
QC = 256
NQ = F // QC
NTOEP = 4
LN_EPS = 1e-5
RMS_EPS = 1e-5
STEPS = 10


def count(eng, sem, per_group, g, k):
    value = per_group * g + k
    if isinstance(value, int) and value <= 0:
        return
    eng.wait_ge(sem, value)


def nothing(*_):
    pass


def decoder_layer(nc, x, xT, ctx, ctxT, wq, wk, wvT, woT, fT, bias, skip, toep,
                  gate_p, gate_s, up_p, up_s, down_p, down_s, out):
    x_v = x.rearrange("b t f -> t b f")
    out_v = out.rearrange("b t f -> t b f")
    ctx_v = ctx.rearrange("b t f -> t b f")
    xT_v = xT.rearrange("(k p) t -> p k t", p=P)
    ctxT_v = ctxT.rearrange("(k p) t -> p k t", p=P)

    with ExitStack() as stack:
        def sb(name, shape, dt=F32):
            return stack.enter_context(nc.sbuf_tensor(name, shape, dt))

        def sem(name):
            return stack.enter_context(nc.semaphore(name))

        fold_hi = sb("fold_hi", [P, 4, KT, D], F32R)
        fold_lo = sb("fold_lo", [P, 4, KT, D], F32R)
        wv_hi = sb("wv_hi", [P, KT, D], F32R)
        wo_sb = sb("wo_sb", [P, KT, D])
        ffn_hi = sb("ffn_hi", [P, 3, 2, F], F32R)
        ffn_lo = sb("ffn_lo", [P, 3, 2, F], F32R)
        toep_sb = sb("toep_sb", [P, NTOEP, 2 * P])
        ident = sb("ident", [P, P])
        causal = sb("causal", [P, P])
        head_one = sb("head_one", [P, HT, DK])
        skip_mat = sb("skip_mat", [P, CH, CI])
        head_sel = sb("head_sel", [P, HT])
        f_small = sb("f_small", [P, 4, DK])
        b_small = sb("b_small", [P, 6])
        skip_sb = sb("skip_sb", [P, 1])
        minus_half = sb("minus_half", [P, 1])
        act_bias = sb("act_bias", [P, 2])
        with ExitStack() as early:
            def sbe(name, shape, dt=F32):
                return early.enter_context(nc.sbuf_tensor(name, shape, dt))
            wv_sb = sbe("wv_sb", [P, KT, D])
            xT_sb = sbe("xT_sb", [P, KT, T])
            inter = sbe("inter", [P, 2, T])
        wv_lo = sb("wv_lo", [P, KT, D], F32R)
        xT_lo = sb("xT_lo", [P, KT, T], F32R)
        inter_lo = sb("inter_lo", [P, 2, T], F32R)
        xT_hi = sb("xT_hi", [P, KT, T], F32R)
        x_sb = sb("x_sb", [P, NB, D])
        ctxT_sb = sb("ctxT_sb", [P, KT, T])
        res_sb = ctxT_sb[:].rearrange("p k (b t) -> p (k b t)", b=NB).rearrange("p (b f) -> p b f", f=D)
        gate_q = sb("gate_q", [P, 2, T])
        sc_sb = gate_q[:].rearrange("p n (h c) -> p n h c", c=P)
        o_sb = gate_q
        conv_sb = gate_q[:].rearrange("p k (b t) -> p k b t", b=NB)
        qT_sb = sb("qT_sb", [P, KT, T])
        rms_sb = x1T_sb = qT_sb
        kT_sb = sb("kT_sb", [P, KT, T])
        fac_sb = prod_sb = kT_sb
        v_sb = sb("v_sb", [P, NB, HT, 3 * DK])
        ctx_sb = sb("ctx_sb", [P, NB, D])
        mean_sq = sb("mean_sq", [P, NB * H])
        inv_rms = sb("inv_rms", [P, NB * H])
        newton = sb("newton", [P, NB * H])
        ve = sb("ve", [P, 3, NB])
        st = sb("st", [P, 3, NB, 6])
        mv = sb("mv", [P, 3, NB, 2])
        x2_sb = sb("x2_sb", [P, NB, D])
        qbd = sb("qbd", [P, 4, T])
        kv_sb = qbd[:, 0:2, :]
        z_sb = qbd[:, 2:4, :]

        psum = [stack.enter_context(nc.psum_tensor(f"bank{i}", [P, T], F32)) for i in range(8)]
        fb = psum[0:4]
        gate_ps, up_ps = psum[4], psum[5]
        down_ps = psum[6:8]
        skip_ps = x2T_ps = psum[4:6]

        def sems(*names):
            return [sem(n) for n in names]

        ld_fold, ld_wo, ld_factors, ld_small, ld_xT, ld_x, ld_ctxT, ld_ctx, stored = sems(
            "ld_fold", "ld_wo", "ld_factors", "ld_small", "ld_xT", "ld_x", "ld_ctxT", "ld_ctx", "stored")
        ld_w = sems("ld_w_even", "ld_w_odd")
        ld_toep = sems(*[f"ld_toep{i}" for i in range(NTOEP)])
        fold_mm, proj_mm, v_mm, s_mm, o_mm, ms_mm, rT_mm, wo_mm, x1T_mm = sems(
            "fold_mm", "proj_mm", "v_mm", "s_mm", "o_mm", "ms_mm", "rT_mm", "wo_mm", "x1T_mm")
        y_mm, cT_mm, skip_mm, x2T_mm, gate_mm, up_mm, down_mm = sems(
            "y_mm", "cT_mm", "skip_mm", "x2T_mm", "gate_mm", "up_mm", "down_mm")
        foldhi_ready, foldlo_ready, wvhi_ready, wvlo_ready, xhi_ready, xlo_ready = sems(
            "foldhi_ready", "foldlo_ready", "wvhi_ready", "wvlo_ready", "xhi_ready", "xlo_ready")
        q2_ready, v_ready, sq_ready, wide_ready, rT_ready, x1T_ready = sems(
            "q2_ready", "v_ready", "sq_ready", "wide_ready", "rT_ready", "x1T_ready")
        x2hi_ready, gelu_ready, ihi_ready, relu_ready, whi_ready = sems(
            "x2hi_ready", "gelu_ready", "ihi_ready", "relu_ready", "whi_ready")
        dve_const, bd_ready, qk_ready, sm_ready, on_ready, z_ready, conv_ready = sems(
            "dve_const", "bd_ready", "qk_ready", "sm_ready", "on_ready", "z_ready", "conv_ready")
        ms_ready, newton_step, rms_ready, half_ready, sk_ready, x2lo_ready, inter_ready, ilo_ready = sems(
            "ms_ready", "newton_step", "rms_ready", "half_ready", "sk_ready", "x2lo_ready", "inter_ready", "ilo_ready")
        code_ready, sign_ready, scale_ready, sum4_ready, wlo_ready = sems(
            "code_ready", "sign_ready", "scale_ready", "sum4_ready", "wlo_ready")
        y_ready, st_ready, mv_ready, ve_ready, ln_ready = (
            sems(*[f"{n}{i}" for i in (1, 2, 3)]) for n in ("y_ready", "st_ready", "mv_ready", "ve_ready", "ln_ready"))
        x1_ready, x2_ready, res_ready = ln_ready
        spread_ready = sems("spread_even_ready", "spread_odd_ready")
        filled, const_ready, pool_mask, kv_ready, prod_ready, sum6_ready, deq_ready = sems(
            "filled", "const_ready", "pool_mask", "kv_ready", "prod_ready", "sum6_ready", "deq_ready")
        last_mm, last_stored = sems("last_mm", "last_stored")
        rstd_ready = sems("rstd_ready1", "rstd_ready2", "rstd_ready3")

        raw_w = sb("raw_w", [P, 2, QC], I32)
        raw_s = sb("raw_s", [P, 2, QC])
        code = sb("code", [P, 3, QC], I32)
        sgn_scale = sb("sgn_scale", [P, 3, QC])
        relu4 = sb("relu4", [P, 2, QC])
        relu6 = sb("relu6", [P, 2, QC])
        weight = sb("weight", [P, 2, QC])
        x2T_hi = sb("x2T_hi", [P, 2, T], F32R)
        x2T_lo = sb("x2T_lo", [P, 2, T], F32R)
        inter_hi = sb("inter_hi", [P, 2, T], F32R)
        raw_q = ctxT_sb
        raw_k = x1T_sb
        f_bd = gate_q[:].rearrange("p k (b s) -> p (k b) s", s=P)[:, 0:4, :]
        raw_wq = raw_q[:].rearrange("p k (a n) -> p (k a) n", n=D)[:, 0:KT, :]
        raw_wk = raw_k[:].rearrange("p k (a n) -> p (k a) n", n=D)[:, 0:KT, :]

        def channels(tile, kt, h):
            return tile[:, kt, :].rearrange("p (b c) -> p b c", c=S)[:, :, h * CI:(h + 1) * CI]

        def pairs(tile, i):
            return tile[:, i, :].rearrange("p (k b j i) -> p k b j i", k=KT, b=NB, i=CI)

        units = [(m, c) for c in range(NQ) for m in range(3)]
        NU = 2 * len(units)

        packed = [(gate_p, gate_s), (up_p, up_s), (down_p, down_s)]
        scores = [("score", u) for u in range(17)]
        conv = [("conv", h) for h in range(CH)]
        slots = [[] for _ in range(NT)]
        for n in range(4):
            slots[n] = scores[4 * n:4 * n + 4]
        pause = ("pause", 0)
        slots[4] = [scores[16], ("squares", 0), ("squares", 1)]
        slots[5] = [("sums", 0), ("sums", 1), ("rms", 0)]
        slots[6] = [pause, pause, ("wide", 0)]
        slots[7] = [("factor", 0), pause, pause]
        slots[8] = [("outproj", 0), ("outproj", 1), pause]
        slots[9] = [("norm", 0), pause, ("x1T", 0)]
        slots[10] = [pause, pause, conv[0]]
        for n in range(5):
            slots[11 + n] = conv[3 * n + 1:3 * n + 4]

        def with_piece(name, k):
            return name in ("rms", "wide", "factor", "norm") or name == "score" and k % 2 == 1

        SECOND = [(1, 1, 1), (1, 1, 1), (1, 0, 1), (1, 0, 1), (1, 0, 1), (1, 1, 0), (0, 1, 1), (1, 1, 1), (1, 0, 1),
                  (1, 0, 1), (0, 1, 1), (0, 1, 1), (1, 0, 0), (1, 1, 1), (1, 0, 1), (1, 0, 1)]
        START = 1
        FIRST = START + 4 + sum(with_piece(*stage) for slot in slots for stage in slot)
        UNITS_FIRST = FIRST // 2 + 2

        def schedule(eng, turn, front, gate, up, down, unpack, finish):
            pieces = iter(range(NU + 4))

            def beside(times=1):
                for _ in range(times):
                    for n in pieces:
                        unpack(n)
                        break

            def run(g, stages):
                for name, k in stages:
                    if name in front:
                        front[name](g, k)

            def slot(prev, g, s, times=(0, 0, 0)):
                each = -(-len(slots[s]) // 3)
                for i, part in enumerate((gate, up, down)):
                    beside(times[i])
                    part(prev, s)
                    if g is not None:
                        run(g, slots[s][i * each:(i + 1) * each])

            beside(START)
            turn(None, None, 0, lambda pair: beside(1))
            for s in range(NT):
                for stage in slots[s]:
                    run(0, [stage])
                    if with_piece(*stage):
                        beside()
            turn(None, 0, 1, lambda pair: beside(pair // 2))
            for s in range(NT):
                slot(0, 1, s, SECOND[s])
            with eng.Fori(2, G) as g:
                turn(g - 2, g - 1, g)
                for s in range(NT):
                    slot(g - 1, g, s)
            turn(G - 2, G - 1, None)
            for s in range(NT):
                slot(G - 1, None, s)
            finish()

        def spread_waits(eng, g, u):
            mt, hc, b = u // 8, u // 4 % 2, u % 4
            count(eng, qk_ready, 4, g, 2 * mt + 1)
            if u >= 4:
                count(eng, s_mm, 16, g, u - 3)
            elif u < 2:
                count(eng, y_mm, 16, g, 0)
                count(eng, conv_ready, 16, g, 0)
            return mt, hc, b

        block = stack.enter_context(nc.Block())

        @block.sync
        def _(sp):
            def load_xT(g, tok):
                count(sp, v_mm, 2, g, 0)
                sp.dma_start(xT_sb[:], xT_v[:, :, bass.ds(tok, T)]).then_inc(ld_xT, 16)

            def load(g):
                tok, seq = (g * T, g * NB) if isinstance(g, int) else (sp.snap(g * T), sp.snap(g * NB))
                if not isinstance(g, int) or g:
                    load_xT(g, tok)
                if isinstance(g, int):
                    sp.wait_ge(*((z_ready, 16 * g) if g else (fold_mm, 4)))
                else:
                    count(sp, stored, 16, g, -16)
                sp.dma_start(ctxT_sb[:], ctxT_v[:, :, bass.ds(tok, T)]).then_inc(ld_ctxT, 16)
                count(sp, x2_ready, NB, g, 0)
                sp.dma_start(x_sb[:], x_v[:, bass.ds(seq, NB), :]).then_inc(ld_x, 16)
                sp.dma_start(ctx_sb[:], ctx_v[:, bass.ds(seq, NB), :]).then_inc(ld_ctx, 16)

            sp.dma_start(raw_wq, wq.rearrange("(k p) n -> p k n", p=P)).then_inc(ld_fold, 16)
            sp.dma_start(raw_wk, wk.rearrange("(k p) n -> p k n", p=P)).then_inc(ld_fold, 16)

            load_xT(0, 0)

            def fetch(u):
                m, c = units[u]
                codes, scales = packed[m]
                sp.dma_start(raw_w[:, u % 2, :], codes[:, c * QC:(c + 1) * QC]).then_inc(ld_w[u % 2], 16)
                src = scales[:, c * QC:(c + 1) * QC].unsqueeze(1).broadcast_to([HT, P // HT, QC])
                sp.dma_start(raw_s[:, u % 2, :], src).then_inc(ld_w[u % 2], 16)

            fetch(0)
            fetch(1)
            load(0)
            for u in range(2, len(units)):
                if u == UNITS_FIRST:
                    load(1)
                sp.wait_ge(scale_ready, 2 * u - 2)
                fetch(u)
            with sp.Fori(2, G) as g:
                load(g)
            for j in range(2):
                sp.wait_ge(res_ready, NB * (G - 1) + 2 * j + 2)
                pair = slice(2 * j, 2 * j + 2)
                at = (G - 1) * NB + 2 * j
                sp.dma_start(out_v[:, at:at + 2, :], res_sb[:, pair]).then_inc(last_stored, 16)
            sp.wait_ge(stored, 16 * (G - 1))
            sp.wait_ge(last_stored, 32)

        @block.gpsimd
        def _(pool):
            nc.gpsimd.memset(ident[:], 0.0).then_inc(filled, 1)
            nc.gpsimd.memset(causal[:], 1.0).then_inc(filled, 1)
            nc.gpsimd.memset(head_one[:], 1.0).then_inc(filled, 1)
            nc.gpsimd.memset(skip_mat[:], 1.0).then_inc(filled, 1)
            nc.gpsimd.memset(minus_half[:], -0.5).then_inc(filled, 1)
            nc.gpsimd.memset(v_sb[:], 0.0).then_inc(filled, 1)
            nc.gpsimd.memset(act_bias[:, 0:1], -0.5).then_inc(filled, 1)
            nc.gpsimd.memset(act_bias[:, 1:2], -1.5).then_inc(filled, 1)
            pool.wait_ge(filled, 8)
            masks = ((head_one, HT, DK), (skip_mat, CH, CI))
            for tile, n, w in masks:
                nc.gpsimd.affine_select(out=tile[:], in_=tile[:], compare_op=ALU.is_ge, fill=0.0, base=0,
                                        pattern=[[-w, n], [0, w]], channel_multiplier=1).then_inc(pool_mask, 1)
            pool.wait_ge(pool_mask, 2)
            for tile, n, w in masks:
                nc.gpsimd.affine_select(out=tile[:], in_=tile[:], compare_op=ALU.is_ge, fill=0.0, base=w - 1,
                                        pattern=[[w, n], [0, w]], channel_multiplier=-1).then_inc(const_ready, 1)
            nc.gpsimd.affine_select(out=ident[:], in_=ident[:], compare_op=ALU.not_equal, fill=1.0,
                                    base=0, pattern=[[-1, P]], channel_multiplier=1).then_inc(const_ready, 1)
            nc.gpsimd.affine_select(out=causal[:], in_=causal[:], compare_op=ALU.is_ge, fill=0.0,
                                    base=0, pattern=[[1, P]], channel_multiplier=-1).then_inc(const_ready, 1)

            pool.wait_ge(dve_const, 7)

            def unpack(step):
                n = step - 2
                if n < 0 or n >= NU:
                    return
                pool.wait_ge(relu_ready, 2 * n + 2)
                pool.wait_ge(sum4_ready, n + 1)
                nc.gpsimd.tensor_tensor(relu6[:, n % 2], relu4[:, n % 2], relu6[:, n % 2], ALU.subtract)\
                    .then_inc(sum6_ready, 1)
                pool.wait_ge(sum6_ready, n + 1)
                pool.wait_ge(scale_ready, n + 1)
                if n >= 2:
                    pool.wait_ge(whi_ready, n - 1)
                    pool.wait_ge(wlo_ready, n - 1)
                nc.gpsimd.tensor_tensor(weight[:, n % 2], relu6[:, n % 2], sgn_scale[:, n % 3], ALU.mult)\
                    .then_inc(deq_ready, 1)

            def rstd(g, ln):
                for j in range(2):
                    count(pool, ve_ready[ln], 2, g, j + 1)
                    nc.gpsimd.tensor_tensor(ve[:, ln, 2 * j:2 * j + 2], ve[:, ln, 2 * j:2 * j + 2],
                                            minus_half[:].broadcast_to([P, 2]), ALU.pow).then_inc(rstd_ready[ln], 1)

            def spread(g, u):
                mt, hc, b = spread_waits(pool, g, u)
                nc.gpsimd.tensor_tensor(qbd[:, u % 4, :].rearrange("p (h c) -> p h c", c=S),
                                        qT_sb[:, mt, b * S:(b + 1) * S].unsqueeze(1).broadcast_to([P, 4, S]),
                                        head_sel[:, 4 * hc:4 * hc + 4].unsqueeze(2).broadcast_to([P, 4, S]),
                                        ALU.mult).then_inc(spread_ready[1], 1)

            def score(g, u):
                if u + 2 < 16 and u % 2:
                    spread(g, u + 2)

            def norm(g, _):
                rstd(g, 0)

            def x1T(g, _):
                products(g, 0)

            def skip_products(g, j):
                count(pool, x1_ready, NB, g, NB)
                count(pool, ld_ctx, 16, g, 16)
                count(pool, s_mm, 16, g, 16)
                nc.gpsimd.tensor_tensor(prod_sb[:, j, :], x_sb[:, 2 * j:2 * j + 2].rearrange("p b f -> p (b f)"),
                                        ctx_sb[:, 2 * j:2 * j + 2].rearrange("p b f -> p (b f)"), ALU.mult)\
                    .then_inc(prod_ready, 1)

            def conv(g, h):
                if h < CH - 1:
                    products(g, h + 1)
                if h in (CH - 4, CH - 2):
                    skip_products(g, h // 2 + 2 - CH // 2)

            def products(g, h):
                if h == 0:
                    count(pool, ld_ctxT, 16, g, 16)
                    count(pool, s_mm, 16, g, 16)
                if h >= 2:
                    count(pool, y_mm, 16, g, h - 1)
                for kt in range(KT):
                    if h == 0:
                        count(pool, x1T_ready, 2, g, kt + 1)
                    v_i = channels(x1T_sb, kt, h).unsqueeze(2).broadcast_to([P, NB, CI, CI])
                    c_j = channels(ctxT_sb, kt, h).unsqueeze(3).broadcast_to([P, NB, CI, CI])
                    nc.gpsimd.tensor_tensor(pairs(kv_sb, h % 2)[:, kt], v_i, c_j, ALU.mult).then_inc(kv_ready, 1)

            def turn(done, prev, g, beside=nothing):
                if prev is not None:
                    rstd(prev, 1)
                if g is not None:
                    for pair in range(4):
                        beside(pair)
                    spread(g, 1)
                if done is not None:
                    rstd(done, 2)
                    at = done * NB if isinstance(done, int) else pool.snap(done * NB)
                    count(pool, res_ready, NB, done, NB)
                    pool.dma_start(out_v[:, bass.ds(at, NB), :], res_sb).then_inc(stored, 16)

            schedule(pool, turn, {"score": score, "norm": norm, "x1T": x1T, "conv": conv}, nothing, nothing, nothing, unpack,
                     lambda: rstd(G - 1, 2))

        @block.scalar
        def _(act):
            def split_x(g):
                for kt in range(KT):
                    count(act, ld_xT, 16, g, 16)
                    nc.scalar.activation(xT_hi[:, kt, :], xT_sb[:, kt, :], ACT.Copy)\
                        .then_inc(xhi_ready, 1)

            act.dma_start(f_small[:], fT.rearrange("n p e -> p n e")).then_inc(ld_factors, 16)
            act.dma_start(b_small[:, 0:5], bias).then_inc(ld_small, 16)
            act.dma_start(skip_sb[:], skip).then_inc(ld_small, 16)
            act.dma_start(wv_sb[:], wvT.rearrange("(k p) n -> p k n", p=P)).then_inc(ld_wo, 16)
            act.dma_start(wo_sb[:], woT.rearrange("(k p) n -> p k n", p=P)).then_inc(ld_wo, 16)
            for i in range(4):
                if i == 2:
                    split_x(0)
                act.wait_ge(fold_mm, i + 1)
                nc.scalar.activation(fold_hi[:, i].rearrange("p k n -> p (k n)"), fb[i][:, :], ACT.Copy)\
                    .then_inc(foldhi_ready, 1)
            act.wait_ge(ld_wo, 32)
            nc.scalar.activation(wv_hi[:], wv_sb[:], ACT.Copy).then_inc(wvhi_ready, 1)
            act.wait_ge(filled, 8)
            act.wait_ge(bd_ready, 1)

            def unpack(step):
                if 1 <= step <= NU:
                    n = step - 1
                    act.wait_ge(code_ready, n + 1)
                    if n >= 2:
                        act.wait_ge(sum6_ready, n - 1)
                    nc.scalar.activation(relu4[:, n % 2], code[:, n % 3], ACT.Relu, bias=act_bias[:, 0:1],
                                         scale=0.125)\
                        .then_inc(relu_ready, 1)
                    if n >= 2:
                        act.wait_ge(deq_ready, n - 1)
                    nc.scalar.activation(relu6[:, n % 2], code[:, n % 3], ACT.Relu, bias=act_bias[:, 1:2],
                                         scale=0.25).then_inc(relu_ready, 1)
                if 3 <= step <= NU + 2:
                    q = step - 3
                    act.wait_ge(deq_ready, q + 1)
                    (m, c), w = units[q // 2], q % 2
                    nc.scalar.activation(ffn_hi[:, m, w, c * QC:(c + 1) * QC], weight[:, q % 2], ACT.Copy)\
                        .then_inc(whi_ready, 1)

            def proj(g, p):
                is_q = p % 4 == 0
                count(act, proj_mm, 8, g, p + 1)
                count(act, qk_ready, 4, g, p // 2 - 1)
                if p < 4:
                    count(act, cT_mm, 2, g, 0)
                nc.scalar.activation(gate_q[:, (p // 2) % 2, :], fb[0][:, :], ACT.Identity,
                                     scale=DK ** -0.5 if is_q else 1.0,
                                     bias=b_small[:, 5:6] if is_q else b_small[:, 3:4]).then_inc(q2_ready, 1)

            def vproj(g, j):
                count(act, v_mm, 2, g, j + 1)
                count(act, o_mm, 16, g, 0)
                nc.scalar.activation(
                    v_sb[:, 2 * j:2 * j + 2].rearrange("p b t (w e) -> p (b t) w e", e=DK)[:, :, 0:3:2, :],
                    fb[2 + j][:, :].rearrange("p (n w e) -> p n w e", w=2, e=DK), ACT.Copy).then_inc(v_ready, 1)

            def spread(g, u):
                mt, hc, b = spread_waits(act, g, u)
                for k in range(4):
                    h = 4 * hc + k
                    last = nc.scalar.activation(qbd[:, u % 4, k * P:(k + 1) * P], qT_sb[:, mt, b * S:(b + 1) * S],
                                                ACT.Copy, scale=head_sel[:, h:h + 1])
                last.then_inc(spread_ready[0], 1)

            def score(g, u):
                if u + 2 < 16 and u % 2 == 0:
                    spread(g, u + 2)

            def squares(g, mt):
                count(act, o_mm, 16, g, 8 * mt + 8)
                count(act, spread_ready[0], 8, g, 4 * mt + 4)
                count(act, spread_ready[1], 8, g, 4 * mt + 4)
                nc.scalar.activation(rms_sb[:, mt, :], fb[2 + mt][:, :], ACT.Square).then_inc(sq_ready, 1)

            def wide(g, _):
                count(act, ms_mm, 2, g, 2)
                count(act, rms_ready, 1, g, 1)
                nc.scalar.activation(rms_sb[:].rearrange("p k (n e) -> p (k n) e", e=DK),
                                     inv_rms[:].unsqueeze(2).broadcast_to([P, NB * H, DK]), ACT.Copy)\
                    .then_inc(wide_ready, 1)

            def factor(g, _):
                for mt in range(KT):
                    count(act, rT_mm, 2, g, mt + 1)
                    nc.scalar.activation(fac_sb[:, mt, :], fb[mt][:, :], ACT.Copy).then_inc(rT_ready, 1)

            def x1T(g, _):
                for j in range(KT):
                    count(act, x1T_mm, 2, g, j + 1)
                    nc.scalar.activation(x1T_sb[:, j, :], fb[2 + j][:, :], ACT.Copy).then_inc(x1T_ready, 1)

            def load_filter(g, h):
                if h < NTOEP - 1:
                    count(act, y_mm, 16, g, 0)
                else:
                    count(act, y_mm, 16, g, h - NTOEP + 1)
                act.dma_start(toep_sb[:, h % NTOEP, :], toep[h]).then_inc(ld_toep[h % NTOEP], 16)

            def conv(g, h):
                if h + NTOEP - 1 < CH:
                    load_filter(g, h + NTOEP - 1)

            def norm(g, _):
                for h in range(NTOEP - 1):
                    load_filter(g, h)

            def turn(done, prev, g, beside=nothing):
                if g is not None:
                    if not isinstance(g, int) or g:
                        split_x(g)
                    for p in range(0, 8, 2):
                        proj(g, p)
                        beside(p // 2)
                    spread(g, 0)
                    vproj(g, 0)
                if prev is not None:
                    for w in range(2):
                        count(act, x2T_mm, 2, prev, w + 1)
                        nc.scalar.activation(x2T_hi[:, w, :], x2T_ps[w][:, :], ACT.Copy).then_inc(x2hi_ready, 1)
                if g is not None:
                    vproj(g, 1)

            def gelu(g, n):
                count(act, gate_mm, NT, g, n + 1)
                if n >= 2:
                    count(act, down_mm, NT, g, n - 1)
                nc.scalar.activation(inter[:, n % 2, :], gate_ps[:, :], ACT.Gelu_apprx_tanh).then_inc(gelu_ready, 1)

            def inner_hi(g, n):
                count(act, inter_ready, NT, g, n + 1)
                if n >= 2:
                    count(act, down_mm, NT, g, n - 1)
                nc.scalar.activation(inter_hi[:, n % 2, :], inter[:, n % 2, :], ACT.Copy).then_inc(ihi_ready, 1)

            schedule(act, turn, {"score": score, "squares": squares, "wide": wide, "factor": factor, "x1T": x1T,
                                 "norm": norm, "conv": conv},
                     gelu, inner_hi, nothing, unpack, nothing)

        @block.vector
        def _(dve):
            def split_x(g):
                for kt in range(KT):
                    count(dve, xhi_ready, 2, g, kt + 1)
                    nc.vector.tensor_tensor(xT_lo[:, kt, :], xT_sb[:, kt, :],
                                            xT_hi[:, kt, :].bitcast(F32), ALU.subtract).then_inc(xlo_ready, 1)

            dve.wait_ge(ld_factors, 16)
            dve.wait_ge(const_ready, 4)
            for i in range(4):
                nc.vector.tensor_tensor(f_bd[:, i, :].rearrange("p (h e) -> p h e", e=DK), head_one[:],
                                        f_small[:, i, :].unsqueeze(1).broadcast_to([P, HT, DK]), ALU.mult)\
                    .then_inc(dve_const, 1)
            dve.wait_ge(ld_small, 32)
            nc.vector.tensor_copy(head_sel[:], head_one[:, :, 0]).then_inc(dve_const, 1)
            nc.vector.tensor_scalar(skip_mat[:], skip_mat[:], skip_sb[:, 0:1], None, ALU.mult).then_inc(dve_const, 1)
            nc.vector.tensor_scalar(b_small[:, 5:6], b_small[:, 1:2], DK ** -0.5, None, ALU.mult).then_inc(bd_ready, 1)
            dve.wait_ge(ld_wo, 32)
            nc.vector.tensor_scalar(wo_sb[:], wo_sb[:], b_small[:, 4:5], None, ALU.mult).then_inc(dve_const, 1)
            for i in range(4):
                if i == 2:
                    split_x(0)
                dve.wait_ge(foldhi_ready, i + 1)
                nc.vector.tensor_tensor(fold_lo[:, i].rearrange("p k n -> p (k n)"), fb[i][:, :],
                                        fold_hi[:, i].rearrange("p k n -> p (k n)").bitcast(F32), ALU.subtract)\
                    .then_inc(foldlo_ready, 1)
            dve.wait_ge(wvhi_ready, 1)
            nc.vector.tensor_tensor(wv_lo[:], wv_sb[:], wv_hi[:].bitcast(F32), ALU.subtract)\
                .then_inc(wvlo_ready, 1)
            dve.wait_ge(dve_const, 7)

            def unpack(n):
                if 2 <= n <= NU + 1:
                    q = n - 2
                    dve.wait_ge(relu_ready, 2 * q + 1)
                    nc.vector.scalar_tensor_tensor(relu4[:, q % 2], code[:, q % 3], -0.125, relu4[:, q % 2],
                                                   ALU.mult, ALU.subtract).then_inc(sum4_ready, 1)
                if n >= 4:
                    q = n - 4
                    (m, c), w = units[q // 2], q % 2
                    dve.wait_ge(whi_ready, q + 1)
                    nc.vector.tensor_tensor(ffn_lo[:, m, w, c * QC:(c + 1) * QC], weight[:, q % 2],
                                            ffn_hi[:, m, w, c * QC:(c + 1) * QC].bitcast(F32), ALU.subtract)\
                        .then_inc(wlo_ready, 1)
                if n < NU:
                    u, w = n // 2, n % 2
                    dve.wait_ge(ld_w[u % 2], 32 * (u // 2 + 1))
                    if n >= 3:
                        dve.wait_ge(relu_ready, 2 * n - 4)
                        dve.wait_ge(deq_ready, n - 2)
                    nc.vector.tensor_scalar(code[:, n % 3], raw_w[:, u % 2], 4 * w, 7, ALU.logical_shift_right,
                                            ALU.bitwise_and).then_inc(code_ready, 1)
                    nc.vector.tensor_scalar(sgn_scale[:, n % 3].bitcast(I32), raw_w[:, u % 2], 4 * w, 8, ALU.logical_shift_right,
                                            ALU.bitwise_and).then_inc(sign_ready, 1)
                    dve.wait_ge(sign_ready, n + 1)
                    nc.vector.scalar_tensor_tensor(sgn_scale[:, n % 3], sgn_scale[:, n % 3].bitcast(I32), 4.0, raw_s[:, u % 2],
                                                   ALU.subtract, ALU.mult).then_inc(scale_ready, 1)

            def proj(g, p):
                mt, is_q = p // 4, p % 4 == 1
                count(dve, proj_mm, 8, g, p + 1)
                count(dve, q2_ready, 4, g, p // 2 + 1)
                if is_q:
                    count(dve, on_ready, 2, g, 0)
                else:
                    count(dve, skip_mm, 2, g, 0)
                nc.vector.scalar_tensor_tensor((qT_sb if is_q else kT_sb)[:, mt, :], fb[1][:, :],
                                               b_small[:, 0:1] if is_q else b_small[:, 2:3],
                                               gate_q[:, (p // 2) % 2, :], ALU.add, ALU.mult).then_inc(qk_ready, 1)

            def score(g, u):
                if u == 16:
                    return
                count(dve, s_mm, 16, g, u + 1)
                count(dve, o_mm, 16, g, u - 1)
                nc.vector.tensor_tensor(sc_sb[:, u % 2], fb[u % 2][:, :].rearrange("p (h c) -> p h c", c=P),
                                        causal[:].unsqueeze(1).broadcast_to([P, 4, P]), ALU.mult).then_inc(sm_ready, 1)

            def rms(g, _):
                count(dve, ms_mm, 2, g, 2)
                if not isinstance(g, int) or g:
                    count(dve, wide_ready, 1, g, 0)
                nc.vector.tensor_scalar(mean_sq[:], fb[0][:, 0:NB * H], 1.0 / DK, RMS_EPS, ALU.mult, ALU.add)\
                    .then_inc(ms_ready, 1)
                count(dve, ms_ready, 1, g, 1)
                nc.vector.tensor_scalar(newton[:].bitcast(I32), mean_sq[:].bitcast(I32), 1, None,
                                        ALU.logical_shift_right).then_inc(newton_step, 1)
                count(dve, newton_step, STEPS, g, 1)
                nc.vector.tensor_scalar(inv_rms[:].bitcast(I32), newton[:].bitcast(I32), -1, 0x5f3759df,
                                        ALU.mult, ALU.add).then_inc(newton_step, 1)
                for i in range(3):
                    count(dve, newton_step, STEPS, g, 3 * i + 2)
                    nc.vector.tensor_tensor(newton[:], inv_rms[:], inv_rms[:], ALU.mult).then_inc(newton_step, 1)
                    count(dve, newton_step, STEPS, g, 3 * i + 3)
                    nc.vector.scalar_tensor_tensor(newton[:], newton[:], -0.5, mean_sq[:], ALU.mult, ALU.mult)\
                        .then_inc(newton_step, 1)
                    count(dve, newton_step, STEPS, g, 3 * i + 4)
                    nc.vector.scalar_tensor_tensor(inv_rms[:], newton[:], 1.5, inv_rms[:], ALU.add, ALU.mult)\
                        .then_inc(rms_ready if i == 2 else newton_step, 1)

            def factor(g, _):
                count(dve, o_mm, 16, g, 16)
                for mt in range(KT):
                    count(dve, rT_ready, 2, g, mt + 1)
                    nc.vector.tensor_tensor(o_sb[:, mt, :], fb[2 + mt][:, :], fac_sb[:, mt, :], ALU.mult)\
                        .then_inc(on_ready, 1)

            def stats(g, ln, tile, j):
                for b in (2 * j, 2 * j + 1):
                    if b == 2:
                        count(dve, st_ready[ln], NB, g, 2)
                    nc.vector.bn_stats(st[:, ln, b, :], tile[:, b, :]).then_inc(st_ready[ln], 1)
                if j == 0:
                    return
                for b in (0, 1):
                    nc.vector.bn_aggr(mv[:, ln, b, :], st[:, ln, b, :]).then_inc(mv_ready[ln], 1)
                count(dve, st_ready[ln], NB, g, 4)
                count(dve, mv_ready[ln], NB, g, 2)
                nc.vector.tensor_scalar(ve[:, ln, 0:2], mv[:, ln, 0:2, 1], LN_EPS, None, ALU.add).then_inc(ve_ready[ln], 1)
                for b in (2, 3):
                    nc.vector.bn_aggr(mv[:, ln, b, :], st[:, ln, b, :]).then_inc(mv_ready[ln], 1)
                count(dve, mv_ready[ln], NB, g, NB)
                nc.vector.tensor_scalar(ve[:, ln, 2:4], mv[:, ln, 2:4, 1], LN_EPS, None, ALU.add).then_inc(ve_ready[ln], 1)

            def normalise(g, ln, tile, into):
                for b in range(NB):
                    if b % 2 == 0:
                        count(dve, rstd_ready[ln], 2, g, b // 2 + 1)
                    nc.vector.tensor_scalar(into[:, b, :], tile[:, b, :], mv[:, ln, b, 0:1], ve[:, ln, b:b + 1],
                                            ALU.subtract, ALU.mult).then_inc(ln_ready[ln], 1)

            def outproj(g, j):
                count(dve, wo_mm, 2, g, j + 1)
                count(dve, ld_x, 16, g, 16)
                both = x_sb[:, 2 * j:2 * j + 2].rearrange("p b f -> p (b f)")
                nc.vector.tensor_tensor(both, fb[j][:, :], both, ALU.add).then_inc(y_ready[0], 1)
                count(dve, y_ready[0], 2, g, j + 1)
                stats(g, 0, x_sb, j)

            def norm(g, _):
                normalise(g, 0, x_sb, x_sb)

            def conv(g, h):
                if h:
                    conv_sum(g, h - 1)

            def conv_sum(g, h):
                count(dve, y_mm, 16, g, h + 1)
                count(dve, ld_ctxT, 16, g, 16)
                if h >= 2:
                    count(dve, conv_ready, 16, g, h - 1)
                for lt in range(KT):
                    c_i = channels(ctxT_sb, lt, h).unsqueeze(2).broadcast_to([P, NB, CI, CI])
                    last = nc.vector.tensor_tensor(pairs(z_sb, h % 2)[:, lt],
                                                   fb[h % 2][:, :].rearrange("p (k b j i) -> p k b j i", k=KT, b=NB, i=CI)[:, lt],
                                                   c_i, ALU.mult)
                last.then_inc(z_ready, 1)
                count(dve, z_ready, 16, g, h + 1)
                nc.vector.tensor_reduce(conv_sb[:, :, :, h * CI:(h + 1) * CI], pairs(z_sb, h % 2), AX.X, ALU.add)\
                    .then_inc(conv_ready, 1)

            def x2_half(g, j):
                both = x_sb[:, 2 * j:2 * j + 2].rearrange("p b f -> p (b f)")
                ctx2 = ctx_sb[:, 2 * j:2 * j + 2].rearrange("p b f -> p (b f)")
                count(dve, skip_mm, 2, g, j + 1)
                nc.vector.tensor_tensor(ctx2, skip_ps[j][:, :], ctx2, ALU.mult).then_inc(sk_ready, 1)
                count(dve, cT_mm, 2, g, j + 1)
                nc.vector.tensor_tensor(both, fb[2 + j][:, :], both, ALU.add).then_inc(half_ready, 1)

            def x2_rest(g, j):
                both = x_sb[:, 2 * j:2 * j + 2].rearrange("p b f -> p (b f)")
                ctx2 = ctx_sb[:, 2 * j:2 * j + 2].rearrange("p b f -> p (b f)")
                count(dve, half_ready, 2, g, j + 1)
                count(dve, sk_ready, 2, g, j + 1)
                nc.vector.tensor_tensor(both, both, ctx2, ALU.add).then_inc(y_ready[1], 1)
                count(dve, y_ready[1], 2, g, j + 1)
                stats(g, 1, x_sb, j)

            def total(done):
                count(dve, down_mm, NT, done, NT)
                for j in range(2):
                    nc.vector.tensor_tensor(res_sb[:, 2 * j:2 * j + 2].rearrange("p b f -> p (b f)"), down_ps[j][:, :],
                                            x2_sb[:, 2 * j:2 * j + 2].rearrange("p b f -> p (b f)"), ALU.add)\
                        .then_inc(y_ready[2], 1)

            def turn(done, prev, g, beside=nothing):
                if prev is not None:
                    conv_sum(prev, CH - 1)
                if g is not None:
                    if not isinstance(g, int) or g:
                        split_x(g)
                if done is not None:
                    total(done)
                if prev is not None:
                    x2_half(prev, 0)
                    x2_rest(prev, 0)
                if g is not None:
                    proj(g, 1)
                    beside(0)
                if prev is not None:
                    x2_half(prev, 1)
                if g is not None:
                    proj(g, 3)
                    beside(1)
                if prev is not None:
                    x2_rest(prev, 1)
                if g is not None:
                    proj(g, 5)
                    beside(2)
                if prev is not None:
                    if done is not None:
                        count(dve, y_ready[2], 2, done, 2)
                    normalise(prev, 1, x_sb, x2_sb)
                if g is not None:
                    proj(g, 7)
                    beside(3)
                if done is not None:
                    count(dve, y_ready[2], 2, done, 2)
                    stats(done, 2, res_sb, 0)
                    stats(done, 2, res_sb, 1)
                if prev is not None:
                    for w in range(2):
                        count(dve, x2hi_ready, 2, prev, w + 1)
                        nc.vector.tensor_tensor(x2T_lo[:, w, :], x2T_ps[w][:, :], x2T_hi[:, w, :].bitcast(F32),
                                                ALU.subtract).then_inc(x2lo_ready, 1)
                if done is not None:
                    normalise(done, 2, res_sb, res_sb)

            def split(g, n):
                count(dve, ihi_ready, NT, g, n + 1)
                if n >= 2:
                    count(dve, down_mm, NT, g, n - 1)
                nc.vector.tensor_tensor(inter_lo[:, n % 2, :], inter[:, n % 2, :], inter_hi[:, n % 2, :].bitcast(F32),
                                        ALU.subtract).then_inc(ilo_ready, 1)

            def inner(g, n):
                count(dve, up_mm, NT, g, n + 1)
                count(dve, gelu_ready, NT, g, n + 1)
                nc.vector.tensor_tensor(inter[:, n % 2, :], up_ps[:, :], inter[:, n % 2, :], ALU.mult).then_inc(inter_ready, 1)

            def finish():
                g = G - 1
                dve.wait_ge(stored, 16 * g)
                for j in range(2):
                    pair = slice(2 * j, 2 * j + 2)
                    dve.wait_ge(last_mm, j + 1)
                    nc.vector.tensor_tensor(res_sb[:, pair].rearrange("p b f -> p (b f)"), down_ps[j][:, :],
                                            x2_sb[:, pair].rearrange("p b f -> p (b f)"), ALU.add)\
                        .then_inc(y_ready[2], 1)
                    dve.wait_ge(y_ready[2], 2 * g + j + 1)
                    for b in (2 * j, 2 * j + 1):
                        nc.vector.bn_stats(st[:, 2, b, :], res_sb[:, b, :]).then_inc(st_ready[2], 1)
                for j in range(2):
                    pair = slice(2 * j, 2 * j + 2)
                    dve.wait_ge(st_ready[2], NB * g + 2 * j + 2)
                    for b in (2 * j, 2 * j + 1):
                        nc.vector.bn_aggr(mv[:, 2, b, :], st[:, 2, b, :]).then_inc(mv_ready[2], 1)
                    dve.wait_ge(mv_ready[2], NB * g + 2 * j + 2)
                    nc.vector.tensor_scalar(ve[:, 2, pair], mv[:, 2, pair, 1], LN_EPS, None, ALU.add)\
                        .then_inc(ve_ready[2], 1)
                for b in range(NB):
                    dve.wait_ge(rstd_ready[2], 2 * g + b // 2 + 1)
                    nc.vector.tensor_scalar(res_sb[:, b, :], res_sb[:, b, :], mv[:, 2, b, 0:1], ve[:, 2, b:b + 1],
                                            ALU.subtract, ALU.mult).then_inc(res_ready, 1)

            schedule(dve, turn, {"score": score, "rms": rms, "factor": factor, "outproj": outproj, "norm": norm,
                                 "conv": conv}, nothing, inner, split, unpack, finish)

        @block.tensor
        def _(pe):
            pe.wait_ge(ld_fold, 32)
            for i in range(4):
                pe.wait_ge(dve_const, i + 1)
                raw = raw_wq if i < 2 else raw_wk
                for kt in range(KT):
                    for mt in range(KT):
                        at = kt * D + mt * P
                        last = nc.tensor.matmul(fb[i][:, at:at + P], raw[:, mt, kt * P:(kt + 1) * P], f_bd[:, i, :],
                                                start=True, stop=True)
                last.then_inc(fold_mm, 1)
            pe.wait_ge(ld_wo, 32)
            pe.wait_ge(dve_const, 7)

            def split_mm(ps, w_hi, w_lo, x_hi, x_lo, start, stop):
                nc.tensor.matmul(ps, w_hi, x_lo, start=start, stop=False, skip_group_check=True)
                nc.tensor.matmul(ps, w_lo, x_hi, start=False, stop=False, skip_group_check=True)
                return nc.tensor.matmul(ps, w_hi, x_hi, start=False, stop=stop, skip_group_check=True)

            def proj(g, p):
                mt, is_k, first = p // 4, p % 4 // 2, p % 2
                if p == 0:
                    count(pe, z_ready, 16, g, 0)
                if isinstance(g, int) and g == 0:
                    pe.wait_ge(foldlo_ready, 2 if p < 2 else 4)
                if first:
                    count(pe, qk_ready, 4, g, p // 2)
                else:
                    count(pe, q2_ready, 4, g, p // 2)
                i = 2 * is_k + (0 if first else 1)
                cols = slice(mt * P, (mt + 1) * P)
                for kt in range(KT):
                    if p == 0:
                        count(pe, xlo_ready, 2, g, kt + 1)
                    last = split_mm(fb[first][:, :], fold_hi[:, i, kt, cols], fold_lo[:, i, kt, cols],
                                    xT_hi[:, kt, :], xT_lo[:, kt, :], kt == 0, kt == KT - 1)
                last.then_inc(proj_mm, 1)

            def vproj(g, j):
                if j == 0:
                    count(pe, half_ready, 2, g, 0)
                    if isinstance(g, int) and g == 0:
                        pe.wait_ge(wvlo_ready, 1)
                for b in (2 * j, 2 * j + 1):
                    for kt in range(KT):
                        toks = slice(b * S, (b + 1) * S)
                        last = split_mm(fb[2 + j][:, (b % 2) * D:(b % 2 + 1) * D], xT_hi[:, kt, toks],
                                        xT_lo[:, kt, toks], wv_hi[:, kt, :], wv_lo[:, kt, :],
                                        kt == 0, kt == KT - 1)
                last.then_inc(v_mm, 1)

            def score(g, u):
                if u < 16:
                    mt, hc, b = u // 8, u // 4 % 2, u % 4
                    if u == 0:
                        count(pe, qk_ready, 4, g, 4)
                    count(pe, spread_ready[u % 2], 8, g, u // 2 + 1)
                    if u >= 2:
                        count(pe, sm_ready, 16, g, u - 1)
                    nc.tensor.matmul(fb[u % 2][:, :].rearrange("p (h c) -> p h c", c=P),
                                     kT_sb[:, mt, b * S:(b + 1) * S],
                                     qbd[:, u % 4, :].rearrange("p (h c) -> p h c", c=P),
                                     start=True, stop=True).then_inc(s_mm, 1)
                if u >= 1:
                    u -= 1
                    mt, hc, b = u // 8, u // 4 % 2, u % 4
                    count(pe, v_ready, 2, g, 2)
                    count(pe, sm_ready, 16, g, u + 1)
                    for k in range(4):
                        pair, odd = (4 * hc + k) // 2, k % 2
                        last = nc.tensor.matmul(fb[2 + mt][32 * pair:32 * pair + 32, b * S:(b + 1) * S],
                                                v_sb[:, b, 4 * mt + pair, DK * odd:DK * odd + 2 * DK],
                                                sc_sb[:, u % 2, k, :], start=odd == 0, stop=odd == 1)
                    last.then_inc(o_mm, 1)

            def sums(g, mt):
                count(pe, sm_ready, 16, g, 16)
                count(pe, sq_ready, 2, g, mt + 1)
                for b in range(NB):
                    at = b * H + mt * HT
                    last = nc.tensor.matmul(fb[0][:, at:at + HT], rms_sb[:, mt, b * S:(b + 1) * S], head_sel[:],
                                            start=True, stop=True)
                last.then_inc(ms_mm, 1)

            def factor(g, _):
                count(pe, wide_ready, 1, g, 1)
                wide = rms_sb[:].rearrange("p k t -> p (k t)")
                for mt in range(KT):
                    for b in range(NB):
                        at = b * D + mt * P
                        last = nc.tensor.transpose(fb[mt][:, b * S:(b + 1) * S], wide[:, at:at + P], ident[:])
                    last.then_inc(rT_mm, 1)

            def outproj(g, j):
                count(pe, on_ready, 2, g, 2)
                for b in (2 * j, 2 * j + 1):
                    for kt in range(KT):
                        last = nc.tensor.matmul(fb[j][:, (b % 2) * D:(b % 2 + 1) * D],
                                                o_sb[:, kt, b * S:(b + 1) * S], wo_sb[:, kt, :],
                                                start=kt == 0, stop=kt == KT - 1)
                last.then_inc(wo_mm, 1)

            def x1T(g, _):
                for b in range(NB):
                    count(pe, x1_ready, NB, g, b + 1)
                    for j in range(KT):
                        last = nc.tensor.transpose(fb[2 + j][:, b * S:(b + 1) * S], x_sb[:, b, j * P:(j + 1) * P],
                                                   ident[:])
                        if b == NB - 1:
                            last.then_inc(x1T_mm, 1)

            def conv(g, h):
                count(pe, ld_toep[h % NTOEP], 16 * CH // NTOEP, g, 16 * (h // NTOEP + 1))
                count(pe, kv_ready, 32, g, 2 * h + 1)
                if h >= 2:
                    count(pe, z_ready, 16, g, h - 1)
                n = NB * CI * CI
                diag, off = toep_sb[:, h % NTOEP, 0:P], toep_sb[:, h % NTOEP, P:2 * P]
                kv = kv_sb[:, h % 2, :]
                nc.tensor.matmul(fb[h % 2][:, 0:n], diag, kv[:, 0:n], start=True, stop=True)
                nc.tensor.matmul(fb[h % 2][:, n:2 * n], off, kv[:, 0:n], start=True, stop=False)
                count(pe, kv_ready, 32, g, 2 * h + 2)
                nc.tensor.matmul(fb[h % 2][:, n:2 * n], diag, kv[:, n:2 * n], start=False, stop=True).then_inc(y_mm, 1)

            def conv_out(g):
                for j in range(2):
                    count(pe, prod_ready, 2, g, j + 1)
                    nc.tensor.matmul(skip_ps[j][:, :], skip_mat[:].rearrange("p h i -> p (h i)"), prod_sb[:, j, :],
                                     start=True, stop=True).then_inc(skip_mm, 1)
                count(pe, conv_ready, 16, g, 16)
                for j in range(2):
                    for b in (2 * j, 2 * j + 1):
                        for lt in range(KT):
                            at = (b % 2) * D + lt * P
                            last = nc.tensor.transpose(fb[2 + j][:, at:at + P], conv_sb[:, lt, b, :], ident[:])
                    last.then_inc(cT_mm, 1)

            def x2T(g):
                count(pe, sk_ready, 2, g, 2)
                for b in range(NB):
                    count(pe, x2_ready, NB, g, b + 1)
                    for w in range(2):
                        last = nc.tensor.transpose(x2T_ps[w][:, b * S:(b + 1) * S], x2_sb[:, b, w::2], ident[:])
                        if b == NB - 1:
                            last.then_inc(x2T_mm, 1)

            def turn(done, prev, g, beside=nothing):
                if done is not None:
                    down(done, NT - 1)
                if prev is not None:
                    conv_out(prev)
                if g is not None:
                    for p in range(8):
                        proj(g, p)
                    vproj(g, 0)
                if prev is not None:
                    x2T(prev)
                if g is not None:
                    vproj(g, 1)

            def weights_ready(g, n, m):
                if isinstance(g, int) and g == 0 and n % 2 == 0:
                    pe.wait_ge(wlo_ready, 2 * (3 * (n // 2) + m))

            def down(g, n, pair_done=None):
                weights_ready(g, n, 3)
                count(pe, ihi_ready, NT, g, n + 1)
                count(pe, ilo_ready, NT, g, n + 1)
                cols = slice(n // 2 * D, (n // 2 + 1) * D)
                for b in range(NB):
                    toks = slice(b * S, (b + 1) * S)
                    last = split_mm(down_ps[b // 2][:, (b % 2) * D:(b % 2 + 1) * D],
                                    inter_hi[:, n % 2, toks], inter_lo[:, n % 2, toks],
                                    ffn_hi[:, 2, n % 2, cols], ffn_lo[:, 2, n % 2, cols],
                                    n == 0 and b % 2 == 0, n == NT - 1)
                    if pair_done is not None and b % 2:
                        last.then_inc(pair_done, 1)
                if pair_done is None:
                    last.then_inc(down_mm, 1)

            def times_x2(g, n, m, ps, free, done):
                weights_ready(g, n, m + 1)
                if n:
                    count(pe, free, NT, g, n)
                cols = slice(n * P, (n + 1) * P)
                for w in range(2):
                    if n == 0 and m == 0:
                        count(pe, x2hi_ready, 2, g, w + 1)
                        count(pe, x2lo_ready, 2, g, w + 1)
                    last = split_mm(ps[:, :], ffn_hi[:, m, w, cols], ffn_lo[:, m, w, cols],
                                    x2T_hi[:, w, :], x2T_lo[:, w, :], w == 0, w == 1)
                last.then_inc(done, 1)

            def gate(g, n):
                times_x2(g, n, 0, gate_ps, gelu_ready, gate_mm)

            def up(g, n):
                times_x2(g, n, 1, up_ps, inter_ready, up_mm)

            def down_before(g, n):
                if n:
                    down(g, n - 1)

            schedule(pe, turn, {"score": score, "sums": sums, "factor": factor, "outproj": outproj, "x1T": x1T,
                                "conv": conv}, gate, up, down_before, nothing, lambda: down(G - 1, NT - 1, last_mm))


def kernel(**inputs):
    import numpy as np
    import concourse.bacc as bacc
    from concourse.bass_utils import run_bass_kernel_spmd

    a = {name.removeprefix("L0_"): np.asarray(v) for name, v in inputs.items()}
    heads = HT
    taps = a["xattn_k"]
    padded = np.concatenate([np.zeros((CH, P - 1), taps.dtype), taps], axis=1)
    toep = padded[:, P - 1 + np.arange(2 * P)[None, :] - np.arange(P)[:, None]]

    def by_input(packed):
        t = packed.reshape(NT // 2, P, 2, -1).transpose(3, 0, 2, 1)
        return t.reshape(t.shape[0], -1)

    def down_rows(packed):
        t = packed.T.reshape(NT // 2, -1, D).transpose(1, 0, 2)
        return t.reshape(t.shape[0], -1)

    arrays = {
        "x": a["x"],
        "xT": a["x"].transpose(2, 0, 1).reshape(D, B * S),
        "ctx": a["ctx_2048"],
        "ctxT": a["ctx_2048"].transpose(2, 0, 1).reshape(D, B * S),
        "wq": a["attn_wq"],
        "wk": a["attn_wk"],
        "wvT": a["attn_wv"].T,
        "woT": a["attn_wo"].T,
        "fT": np.stack([np.tile(a[f"attn_{n}_w"].T, (heads, 1)) for n in ("fq1", "fq2", "fk1", "fk2")]),
        "bias": np.stack([np.tile(a[n], heads) for n in ("attn_fq1_b", "attn_fq2_b", "attn_fk1_b", "attn_fk2_b",
                                                         "attn_norm_w")], axis=1),
        "skip": a["fside_S2_0"].reshape(P, 1),
        "toep": toep,
        "gate_p": by_input(a["ffn_gate_W_packed"]),
        "gate_s": by_input(a["ffn_gate_scales"]),
        "up_p": by_input(a["ffn_up_W_packed"]),
        "up_s": by_input(a["ffn_up_scales"]),
        "down_p": down_rows(a["ffn_down_W_packed"]),
        "down_s": down_rows(a["ffn_down_scales"]),
    }
    arrays = {n: np.ascontiguousarray(v) for n, v in arrays.items()}
    nc = bacc.Bacc("TRN2", target_bir_lowering=False, num_devices=1)
    aps = {n: nc.dram_tensor(f"in_{n}", v.shape, mybir.dt.from_np(v.dtype), kind="ExternalInput").ap()
           for n, v in arrays.items()}
    out = nc.dram_tensor("out_0", (B, S, D), F32, kind="ExternalOutput").ap()
    decoder_layer(nc, **aps, out=out)
    r = run_bass_kernel_spmd(nc, [{f"in_{n}": v for n, v in arrays.items()}], core_ids=[0])
    return r.results[0]["out_0"]
```
